# Optimizing a Trainium2 kernel written in Bass

```python
import numpy as np
import jax
import jax.numpy as jnp

def _softmax(x, axis=-1):
    return jax.nn.softmax(x, axis=axis)

def _gelu(x):
    return jax.nn.gelu(x, approximate=True)

def _silu(x):
    return jax.nn.silu(x)

def _sigmoid(x):
    return jax.nn.sigmoid(x)

def _layernorm(x, axis=-1, eps=1e-05):
    m = jnp.mean(x, axis=axis, keepdims=True)
    v = jnp.var(x, axis=axis, keepdims=True)
    return (x - m) / jnp.sqrt(v + eps)

def _scatter_add(tgt, idx, src, axis=0):
    return tgt.at[idx].add(src)

def _segment_sum(src, seg, n):
    return jax.ops.segment_sum(src, seg, n)
kernel_name = 'mk_flamingo_gated_d1_seqx_r8_166864'

def setup_inputs(seed: int=0):
    np.random.seed(seed)
    _w = jnp.asarray

    def _rec_inputs():
        import jax
        import jax.numpy as jnp
        _rk = jax.random.key(seed)
        x = 7.22e-05 + 1 * jax.random.normal(jax.random.fold_in(_rk, 1), (8, 128, 256), jnp.float32)
        _lenS = 128 - jax.random.randint(jax.random.fold_in(_rk, 7), (8,), 0, max(1, 128 // 4) + 1, jnp.int32)
        _lenS2 = 128 - jax.random.randint(jax.random.fold_in(_rk, 8), (8,), 0, max(1, 128 // 4) + 1, jnp.int32)
        _ctx_2048P = jax.random.normal(jax.random.fold_in(_rk, 11), (8, 16, 256), jnp.float32)
        _ctx_2048c = jax.random.dirichlet(jax.random.fold_in(_rk, 511), 0.3 * jnp.ones((16,), jnp.float32), (8, 128))
        _ctx_2048t = jnp.einsum('bsk,bkd->bsd', _ctx_2048c, _ctx_2048P)
        _ctx_2048t = _ctx_2048t * jax.lax.rsqrt(jnp.mean(jnp.square(_ctx_2048t)) + 1e-12) * 0.953939
        ctx_2048 = 4.13588e-05 + 0.999923 * (_ctx_2048t + 0.3 * jax.random.normal(jax.random.fold_in(_rk, 611), (8, 128, 256), jnp.float32))
        _g = jax.random.normal(jax.random.fold_in(_rk, 9001), (2, 1), jnp.float32)
        _g = jnp.sign(_g) * jnp.maximum(jnp.abs(_g), 1.0) + (_g == 0) * 1.0
        g_xattn = _g[0]
        g_ffn = _g[1]
        return (x, ctx_2048, g_xattn, g_ffn)
    x, ctx_2048, g_xattn, g_ffn = _rec_inputs()

    def _L0_xattn_setup():
        import jax, jax.numpy as jnp
        import numpy as np
        N_HEAD = 8
        ALPHA = 5.0
        EPS = 1e-12

        def _l2norm(x, axis):
            n = jnp.sqrt(jnp.sum(x * x, axis=axis, keepdims=True))
            return x / jnp.maximum(n, EPS)
        key = jax.random.key(seed)
        kq, kk, kv = jax.random.split(key, 3)
        B, D, T = (4, 128, 256)
        q = jax.random.normal(kq, (B, D, T), dtype=jnp.float32)
        k = jax.random.normal(kk, (B, D, T), dtype=jnp.float32)
        v = jax.random.normal(kv, (B, D, T), dtype=jnp.float32)
        return {'q': q, 'k': k, 'v': v}
    _L0_xattn_all = _L0_xattn_setup()
    _L0_xattn_in = {k: v for k, v in _L0_xattn_all.items() if k in ()}
    del _L0_xattn_all

    def _L0_ffn_setup():
        import jax, jax.numpy as jnp
        import numpy as np
        TOP_K = 6
        CAP_FACTOR = 2

        def _moe_block(x2d, wg_router, w_gate, w_up, w_down, ws_gate, ws_up, ws_down):
            T, D = x2d.shape
            E = wg_router.shape[0]
            scores = jax.nn.softmax(x2d @ wg_router.T, axis=-1)
            topk_w, topk_idx = jax.lax.top_k(scores, TOP_K)
            topk_w = topk_w / (jnp.sum(topk_w, axis=-1, keepdims=True) + 1e-20)
            flat_idx = topk_idx.reshape(-1)
            oh = jax.nn.one_hot(flat_idx, E, dtype=jnp.int32)
            pos = jnp.cumsum(oh, axis=0) - 1
            pos_in_e = jnp.take_along_axis(pos, flat_idx[:, None], axis=1)[:, 0]
            C = CAP_FACTOR * (T * TOP_K // E)
            valid = pos_in_e < C
            safe_pos = jnp.where(valid, pos_in_e, 0)
            tok_id = jnp.repeat(jnp.arange(T), TOP_K)
            vmask = valid[:, None].astype(x2d.dtype)
            x_rep = x2d[tok_id] * vmask
            xe = jnp.zeros((E, C, D), x2d.dtype).at[flat_idx, safe_pos].add(x_rep)
            g = jnp.einsum('ecd,edf->ecf', xe, w_gate)
            u = jnp.einsum('ecd,edf->ecf', xe, w_up)
            ye = jnp.einsum('ecf,efd->ecd', jax.nn.silu(g) * u, w_down)
            y_tok = ye[flat_idx, safe_pos] * vmask
            y = jnp.sum(y_tok.reshape(T, TOP_K, D) * topk_w[..., None], axis=1)
            sh = jax.nn.silu(x2d @ ws_gate) * (x2d @ ws_up) @ ws_down
            return y + sh
        key = jax.random.key(seed)
        ks = jax.random.split(key, 9)
        B, S, D, F, E = (1, 256, 256, 176, 32)
        FS = F * 2
        s = 0.02
        return {'hidden_states': jax.random.normal(ks[0], (B, S, D), jnp.float32), 'wg_router': jax.random.normal(ks[1], (E, D), jnp.float32) * s, 'w_gate': jax.random.normal(ks[2], (E, D, F), jnp.float32) * s, 'w_up': jax.random.normal(ks[3], (E, D, F), jnp.float32) * s, 'w_down': jax.random.normal(ks[4], (E, F, D), jnp.float32) * s, 'ws_gate': jax.random.normal(ks[5], (D, FS), jnp.float32) * s, 'ws_up': jax.random.normal(ks[6], (D, FS), jnp.float32) * s, 'ws_down': jax.random.normal(ks[7], (FS, D), jnp.float32) * s}
    _L0_ffn_all = _L0_ffn_setup()
    _L0_ffn_in = {k: v for k, v in _L0_ffn_all.items() if k in ('wg_router', 'w_gate', 'w_up', 'w_down', 'ws_gate', 'ws_up', 'ws_down')}
    del _L0_ffn_all
    return {'x': x, 'ctx_2048': ctx_2048, 'g_xattn': g_xattn, 'g_ffn': g_ffn, 'L0_ffn_wg_router': _L0_ffn_in['wg_router'], 'L0_ffn_w_gate': _L0_ffn_in['w_gate'], 'L0_ffn_w_up': _L0_ffn_in['w_up'], 'L0_ffn_w_down': _L0_ffn_in['w_down'], 'L0_ffn_ws_gate': _L0_ffn_in['ws_gate'], 'L0_ffn_ws_up': _L0_ffn_in['ws_up'], 'L0_ffn_ws_down': _L0_ffn_in['ws_down']}

def reference(x, ctx_2048, g_xattn, g_ffn, L0_ffn_wg_router, L0_ffn_w_gate, L0_ffn_w_up, L0_ffn_w_down, L0_ffn_ws_gate, L0_ffn_ws_up, L0_ffn_ws_down):
    import jax
    import jax.numpy as jnp

    def _L0_xattn_ref(q, k, v):
        import jax, jax.numpy as jnp
        import numpy as np
        N_HEAD = 8
        ALPHA = 5.0
        EPS = 1e-12

        def _l2norm(x, axis):
            n = jnp.sqrt(jnp.sum(x * x, axis=axis, keepdims=True))
            return x / jnp.maximum(n, EPS)
        B, D, Tq = q.shape
        Tk = k.shape[-1]
        Dv = v.shape[-2]
        h = N_HEAD
        d = D // h
        dv = Dv // h
        qh = q.reshape(B, h, d, Tq)
        kh = k.reshape(B, h, d, Tk)
        vh = v.reshape(B, h, dv, Tk)
        qn = _l2norm(qh, axis=-2)
        kn = _l2norm(kh, axis=-2)
        qk = ALPHA * jnp.einsum('bhdq,bhdk->bhqk', qn, kn)
        sm = jax.nn.softmax(qk, axis=-1)
        out = jnp.einsum('bhqk,bhdk->bhdq', sm, vh)
        return out.reshape(B, Dv, Tq)

    def _L0_ffn_ref(hidden_states, wg_router, w_gate, w_up, w_down, ws_gate, ws_up, ws_down):
        import jax, jax.numpy as jnp
        import numpy as np
        TOP_K = 6
        CAP_FACTOR = 2

        def _moe_block(x2d, wg_router, w_gate, w_up, w_down, ws_gate, ws_up, ws_down):
            T, D = x2d.shape
            E = wg_router.shape[0]
            scores = jax.nn.softmax(x2d @ wg_router.T, axis=-1)
            topk_w, topk_idx = jax.lax.top_k(scores, TOP_K)
            topk_w = topk_w / (jnp.sum(topk_w, axis=-1, keepdims=True) + 1e-20)
            flat_idx = topk_idx.reshape(-1)
            oh = jax.nn.one_hot(flat_idx, E, dtype=jnp.int32)
            pos = jnp.cumsum(oh, axis=0) - 1
            pos_in_e = jnp.take_along_axis(pos, flat_idx[:, None], axis=1)[:, 0]
            C = CAP_FACTOR * (T * TOP_K // E)
            valid = pos_in_e < C
            safe_pos = jnp.where(valid, pos_in_e, 0)
            tok_id = jnp.repeat(jnp.arange(T), TOP_K)
            vmask = valid[:, None].astype(x2d.dtype)
            x_rep = x2d[tok_id] * vmask
            xe = jnp.zeros((E, C, D), x2d.dtype).at[flat_idx, safe_pos].add(x_rep)
            g = jnp.einsum('ecd,edf->ecf', xe, w_gate)
            u = jnp.einsum('ecd,edf->ecf', xe, w_up)
            ye = jnp.einsum('ecf,efd->ecd', jax.nn.silu(g) * u, w_down)
            y_tok = ye[flat_idx, safe_pos] * vmask
            y = jnp.sum(y_tok.reshape(T, TOP_K, D) * topk_w[..., None], axis=1)
            sh = jax.nn.silu(x2d @ ws_gate) * (x2d @ ws_up) @ ws_down
            return y + sh
        B, S, D = hidden_states.shape
        x2d = hidden_states.reshape(-1, D)
        out = _moe_block(x2d, wg_router, w_gate, w_up, w_down, ws_gate, ws_up, ws_down)
        return out.reshape(B, S, D)
    x = x + jnp.tanh(g_xattn[0]) * _L0_xattn_ref(_layernorm(x, axis=-1), ctx_2048, ctx_2048)
    x = x + jnp.tanh(g_ffn[0]) * _L0_ffn_ref(_layernorm(x, axis=-1), L0_ffn_wg_router, L0_ffn_w_gate, L0_ffn_w_up, L0_ffn_w_down, L0_ffn_ws_gate, L0_ffn_ws_up, L0_ffn_ws_down)
    return x

_drawn_inputs = setup_inputs


def setup_inputs(seed=0):
    import zlib

    import numpy as np

    out = dict(_drawn_inputs(seed))
    spreads = {}
    factors = {'L0_ffn_wg_router': 8.0,
     'L0_ffn_w_gate': 8.0,
     'L0_ffn_w_up': 8.0,
     'L0_ffn_w_down': 8.0,
     'L0_ffn_ws_gate': 3.72,
     'L0_ffn_ws_up': 3.668,
     'L0_ffn_ws_down': 3.673}
    for name, (base, spread) in spreads.items():
        noise = np.random.default_rng([zlib.crc32(name.encode()), seed]).standard_normal(out[name].shape)
        drawn = base * np.exp(spread * noise) if base else spread * noise
        out[name] = jnp.asarray(drawn.astype(out[name].dtype))
    for name, factor in factors.items():
        out[name] = (out[name] * factor).astype(out[name].dtype)
    return out
```

```python
import concourse.bass as bass
from concourse import mybir
from contextlib import ExitStack

F32 = mybir.dt.float32
BF16 = mybir.dt.bfloat16
U32 = mybir.dt.uint32
I32 = mybir.dt.int32
ALU = mybir.AluOpType
ACT = mybir.ActivationFunctionType
AX = mybir.AxisListType

P = 128
B, T = 8, 256
NH, DH = 8, 16
PAIRS = 4
KC = 2
E, F, TOPK = 32, 176, 6
FH = F // 2
FS = 2 * F
FS_CHUNKS = [(0, 128), (128, 128), (256, 96)]
TOKENS = B * P
CAP = 2 * (TOKENS * TOPK // E)
TILES = 2
ALPHA, LN_EPS = 5.0, 1e-5
NORM_EPS_SQ = 1e-24
SHIFT = 2.0 ** 20
UNSHIFT = 2.0 ** 10
ROW = T + E + 1
W_AT, TOK_AT = T, T + E
RING = 4

C_IDENT, C_BLOCK, C_TRI, C_IOTA, C_EVEN, C_ODD, C_ONES_E, C_ONES_O, C_HALF, C_END = (
    0, 128, 256, 384, 416, 417, 418, 450, 482, 483)


def flamingo_block_kernel(nc, x, ctx_kv, g_xattn, g_ffn, wg_router, w_gate, w_up, w_down,
                          ws_gate, ws_up, ws_down, consts, out):
    slots_dram = nc.dram_tensor("slot_rows", (E * CAP, ROW), F32, kind="Internal").ap()
    acc_dram = [nc.dram_tensor(f"acc{i}", (TOKENS + P, T), F32, kind="Internal").ap() for i in range(TILES)]

    with ExitStack() as ctx:
        def sb(name, shape, dt=F32):
            return ctx.enter_context(nc.sbuf_tensor(name, shape, dt))

        def sem(name):
            return ctx.enter_context(nc.semaphore(name))

        cst = sb("cst", [P, C_END])
        ident = cst[:, C_IDENT:C_IDENT + P]
        head_block = cst[:, C_BLOCK:C_BLOCK + P]
        iota_e = cst[:, C_IOTA:C_IOTA + E]
        even_mask, odd_mask = cst[:, C_EVEN:C_EVEN + 1], cst[:, C_ODD:C_ODD + 1]
        ones_half = [cst[:, C_ONES_E:C_ONES_E + 32], cst[:, C_ONES_O:C_ONES_O + 32]]
        minus_half = cst[:, C_HALF:C_HALF + 1]
        tri = sb("tri", [P, P], BF16)
        ones_bf = sb("ones_bf", [P, P], BF16)
        gates = sb("gates", [P, 2])
        tg = sb("tg", [P, 2])
        wr_sb = sb("wr_sb", [E, T])
        wrT = sb("wrT", [P, KC, E])

        xs = sb("xs", [P, B, T])
        qc = sb("qc", [P, B, 2, T])
        sq = sb("sq", [P, 2, 2 * T])
        ssg = sb("ssg", [P, 2, 2 * T])
        lns = sb("lns", [P, 2, 2 * T])
        rnorm = sb("rnorm", [P, 2, 2 * T])
        qeo = sb("qeo", [P, 2, 2, T])
        kn = sb("kn", [P, 2, T])
        vm = sb("vm", [P, 3, 2, KC, P])
        probs = sb("probs", [P, 2, PAIRS, KC, 2 * T])
        lnden = sb("lnden", [P, 2, T])
        rden = sb("rden", [P, 2, T])
        att = sb("att", [P, 2, T])
        x2 = sb("x2", [P, B, T])
        st1, mv1 = sb("st1", [P, B, 6]), sb("mv1", [P, B, 2])
        st2, mv2 = sb("st2", [P, B, 6]), sb("mv2", [P, B, 2])
        ve1, rstd1 = sb("ve1", [P, B]), sb("rstd1", [P, B])
        ve2, rstd2 = sb("ve2", [P, B]), sb("rstd2", [P, B])
        rows = sb("rows", [P, B, ROW])
        zT = sb("zT", [P, B, KC, P])
        m8, negm, esum, rsum = sb("m8", [P, B, 8]), sb("negm", [P, B]), sb("esum", [P, B]), sb("rsum", [P, B])
        ex, score = sb("ex", [P, B, E]), sb("score", [P, B, E])
        v8, idx8, idxf = sb("v8", [P, B, 8]), sb("idx8", [P, B, 8], U32), sb("idxf", [P, B, TOPK])
        onehot = sb("onehot", [P, 2, TOPK, E])
        chosen = sb("chosen", [P, B, E], BF16)
        before = sb("before", [P, B + 1, E], BF16)
        wsum, wrec, wgate = sb("wsum", [P, B]), sb("wrec", [P, B]), sb("wgate", [P, B])
        posk, over = sb("posk", [P, B, TOPK]), sb("over", [P, B, TOPK])
        prod = sb("prod", [P, 2, TOPK, E])
        dest_f = sb("dest_f", [P, B, TOPK])
        dest = sb("dest", [P, B, TOPK], U32)
        row0 = sb("row0", [P, ROW])
        cmax = sb("cmax", [P, 1])
        flag = sb("flag", [P, 1], I32)

        wsg, wsu = sb("wsg", [P, KC, FS]), sb("wsu", [P, KC, FS])
        wsd = sb("wsd", [P, 3, T])
        sgs, hs = sb("sgs", [P, 2, FS]), sb("hs", [P, 2, FS])
        hsT = sb("hsT", [P, 2, 3, P])
        base = sb("base", [P, 2, T])

        wgu = sb("wgu", [P, RING, KC, 2 * F])
        wd = sb("wd", [FH, RING, 2, T])
        slot = sb("slot", [P, RING, TILES, ROW])
        slotT = sb("slotT", [P, 2, TILES, KC, P])
        wcol = sb("wcol", [P, RING, TILES])
        sg, h = sb("sg", [P, TILES, F]), sb("h", [P, TILES, F])
        hT = sb("hT", [FH, TILES, 2, P])
        ysc = sb("ysc", [P, RING, TILES, T])

        score_ps = ctx.enter_context(nc.psum_tensor("score_ps", [P, 2, KC, 512], F32))
        bank = [score_ps[:, i // 2, i % 2, :] for i in range(4)]
        bank += [ctx.enter_context(nc.psum_tensor(f"bank{i}", [P, 512], F32))[:, :] for i in range(4, 8)]
        num_ps, den_ps, ss_ps = bank[4][:, 0:T], bank[5][:, 0:T], bank[6]
        t_ps = bank[7][:, 0:T].rearrange("p (c n) -> p c n", c=KC)
        logit_ps, pos_ps = bank[6][:, 0:E], bank[6][:, E:2 * E]

        s_in = [sem(f"in_loaded{b}") for b in range(B)]
        s_cst, s_gate, s_wr, s_wsh = sem("consts_loaded"), sem("gates_loaded"), sem("router_loaded"), sem("shared_loaded")
        s_tg, s_setup, s_pconst, s_row0, s_wrps, s_wrT = (sem("tanh_gates"), sem("setup_dve"), sem("setup_pool"),
                                                  sem("empty_row"), sem("router_turned"), sem("router_T"))
        s_init, s_acc0 = sem("slots_cleared"), sem("acc_seeded")
        s_st1, s_mv1, s_ve1, s_rstd1 = sem("ln1_stats"), sem("ln1_mv"), sem("ln1_eps"), sem("ln1_rstd")
        s_q, s_sq, s_ss, s_guard = sem("q_ln"), sem("squares"), sem("sumsq"), sem("sumsq_guarded")
        s_lnss, s_rn, s_qeo, s_kn = sem("ln_sumsq"), sem("rnorm"), sem("q_masked"), sem("k_normed")
        s_vT, s_vm = sem("v_turned"), sem("v_masked")
        s_sc, s_p, s_pv = sem("scores"), sem("probs"), sem("pv_done")
        s_lnden, s_rden, s_att, s_x2 = sem("ln_den"), sem("rden"), sem("att_normed"), sem("x2_ready")
        s_st2, s_mv2, s_ve2, s_rstd2, s_z = sem("ln2_stats"), sem("ln2_mv"), sem("ln2_eps"), sem("ln2_rstd"), sem("z_ready")
        s_zps, s_zT, s_lg = sem("z_turned"), sem("zT_ready"), sem("logits")
        s_m8, s_negm, s_ex, s_rsum, s_score = sem("max8"), sem("neg_max"), sem("exp_logits"), sem("rsum"), sem("router_score")
        s_v8, s_idx, s_idxf, s_oh, s_ch = sem("top8"), sem("top_idx"), sem("top_idx_f"), sem("onehot"), sem("chosen")
        s_wsum, s_weps, s_wrec, s_wg, s_w = sem("wsum"), sem("wsum_eps"), sem("wrec"), sem("wgate"), sem("row_weights")
        s_bef, s_pos, s_prod, s_posk = sem("before"), sem("positions"), sem("pos_prod"), sem("pos_k")
        s_over, s_d1, s_dest, s_scat = sem("over_cap"), sem("dest_raw"), sem("dest"), sem("scattered")
        s_cnt, s_cmax, s_flag = sem("counts"), sem("count_max"), sem("flag")
        s_shps, s_sg_s, s_h_s, s_hps_s, s_hT_s, s_y_s, s_base = (
            sem("sh_gu"), sem("sh_silu"), sem("sh_h"), sem("sh_hturned"), sem("sh_hT"), sem("sh_down"), sem("sh_base"))
        s_seed = [sem(f"sh_seeded{i}") for i in range(2)]
        s_w_in = [sem(f"expert_w_loaded{r}") for r in range(RING)]
        s_x_in = [sem(f"slots_loaded{r}") for r in range(RING)]
        s_xps, s_xT, s_wcol = sem("slots_turned"), sem("slots_T"), sem("slot_weights")
        s_gu = [sem(f"gate_up{t}") for t in range(TILES)]
        s_sg = [sem(f"silu{t}") for t in range(TILES)]
        s_h = [sem(f"hidden{t}") for t in range(TILES)]
        s_hps = [sem(f"hidden_turned{t}") for t in range(TILES)]
        s_hT = [sem(f"hidden_T{t}") for t in range(TILES)]
        s_y = [sem(f"down{t}") for t in range(TILES)]
        s_ys = [sem(f"y_scaled{t}") for t in range(TILES)]
        s_acc = [sem(f"acc_added{t}") for t in range(TILES)]
        s_go = sem("adds_begun")
        o_in, o_xps, o_xT, o_wcol, o_gu, o_sg, o_h, o_hps, o_hT, o_y, o_ys, o_acc = (
            sem("ov_in"), sem("ov_turned"), sem("ov_T"), sem("ov_wcol"), sem("ov_gu"), sem("ov_silu"), sem("ov_h"),
            sem("ov_hturned"), sem("ov_hT"), sem("ov_down"), sem("ov_y"), sem("ov_added"))
        o_free = sem("ov_expert_done")
        s_fin_in, s_fin, s_out = sem("acc_loaded"), sem("out_ready"), sem("out_stored")

        block = ctx.enter_context(nc.Block())

        def slot_rows(e, tiles, first=0):
            v = slots_dram.rearrange("(e t p) r -> e p t r", e=E, p=P)
            if isinstance(e, int):
                return v[e, :, first:first + tiles, :]
            return v[bass.ds(e, 1), :, first:first + tiles, :].rearrange("a p t r -> (a p) t r")

        def of_expert(w, e, pattern, **sizes):
            v = w.rearrange(pattern, **sizes)
            if isinstance(e, int):
                return v[e]
            return v[bass.ds(e, 1)].rearrange("a p c f -> (a p) c f")

        def load_weights(eng, e, r, done):
            eng.dma_start(wgu[:, r, :, 0:F], of_expert(w_gate, e, "e (c p) f -> e p c f", p=P)).then_inc(done, 16)
            eng.dma_start(wgu[:, r, :, F:2 * F], of_expert(w_up, e, "e (c p) f -> e p c f", p=P)).then_inc(done, 16)
            eng.dma_start(wd[:, r, :, :], of_expert(w_down, e, "e (c p) n -> e p c n", p=FH)).then_inc(done, 16)

        def experts(eng, body):
            body(0, 0)
            groups = (E - 1) // RING
            with eng.Fori(0, groups) as i:
                for j in range(RING):
                    body(i * RING + (j + 1), (j + 1) % RING)
            for e in range(1 + groups * RING, E):
                body(e, e % RING)

        @block.sync
        def _(sp):
            sp.dma_start(xs[:, 0, :], x[0]).then_inc(s_in[0], 16)
            sp.dma_start(qc[:, 0, 1, :], ctx_kv[0]).then_inc(s_in[0], 16)
            sp.dma_start(cst[:, :], consts).then_inc(s_cst, 16)
            sp.dma_start(gates[:, 0:1], g_xattn.partition_broadcast(P)).then_inc(s_gate, 16)
            sp.dma_start(gates[:, 1:2], g_ffn.partition_broadcast(P)).then_inc(s_gate, 16)
            sp.dma_start(wr_sb[:, :], wg_router).then_inc(s_wr, 16)
            for b in range(1, B):
                sp.dma_start(xs[:, b, :], x[b]).then_inc(s_in[b], 16)
                sp.dma_start(qc[:, b, 1, :], ctx_kv[b]).then_inc(s_in[b], 16)
            sp.wait_ge(s_row0, 2)
            sp.dma_start(slots_dram.rearrange("(n p) r -> p n r", p=P),
                         row0[:, :].unsqueeze(1).to_broadcast([P, E * CAP // P, ROW])).then_inc(s_init, 16)
            sp.dma_start(acc_dram[0][TOKENS:TOKENS + P, :], row0[:, 0:T]).then_inc(s_acc0, 16)
            sp.dma_start(acc_dram[1].rearrange("(n p) r -> p n r", p=P),
                         row0[:, 0:T].unsqueeze(1).to_broadcast([P, B + 1, T])).then_inc(s_acc0, 16)
            sp.dma_start(wsg[:, :, :], ws_gate.rearrange("(c p) f -> p c f", p=P)).then_inc(s_wsh, 16)
            sp.dma_start(wsu[:, :, :], ws_up.rearrange("(c p) f -> p c f", p=P)).then_inc(s_wsh, 16)
            for c, (f0, n) in enumerate(FS_CHUNKS):
                sp.dma_start(wsd[0:n, c, :], ws_down[f0:f0 + n, :]).then_inc(s_wsh, 16)
            for e in range(RING):
                load_weights(sp, e, e, s_w_in[e])
            for b in range(B):
                sp.wait_ge(s_base, b + 1)
                sp.dma_start(acc_dram[0][b * P:(b + 1) * P, :], base[:, b % 2, :]).then_inc(s_seed[b % 2], 16)
                if b == 0:
                    sp.wait_ge(s_scat, 16 * TOPK * B)
                    for e in range(RING):
                        sp.dma_start(slot[:, e, :, :], slot_rows(e, TILES)).then_inc(s_x_in[e], 16)
            with sp.Fori(0, E // RING - 1) as i:
                for r in range(RING):
                    for t in range(TILES):
                        sp.wait_ge(s_acc[t], i * (16 * RING) + 16 * (r + 1))
                    load_weights(sp, i * RING + (r + RING), r, s_w_in[r])
                    sp.dma_start(slot[:, r, :, :], slot_rows(i * RING + (r + RING), TILES)).then_inc(s_x_in[r], 16)
            for t in range(TILES):
                sp.wait_ge(s_acc[t], 16 * E)
            sp.wait_ge(s_flag, 1)
            n_max = sp.value_load(flag[0:1, 0:1], min_val=0, max_val=TOKENS)
            with sp.If(n_max > TILES * P):
                with sp.Fori(0, E) as e:
                    sp.wait_ge(o_free, e + 1)
                    load_weights(sp, e, 0, o_in)
                    sp.dma_start(slot[:, 0, 0, :], slot_rows(e, 1, TILES).rearrange("p t r -> p (t r)")).then_inc(o_in, 16)
                sp.wait_ge(o_free, E + 1)
            fin = probs[:, :, :, :, :].rearrange("p a b c d -> p (a b c d)")
            half = B // 2
            for c in range(2):
                for t in range(TILES):
                    sp.dma_start(fin[:, (c * 2 + t) * half * T:(c * 2 + t + 1) * half * T].rearrange("p (n r) -> p n r", r=T),
                                 acc_dram[t][c * half * P:(c + 1) * half * P, :].rearrange("(n p) r -> p n r", p=P)
                                 ).then_inc(s_fin_in, 16)
            for c in range(2):
                sp.wait_ge(s_fin, c + 1)
                sp.dma_start(out[c * half:(c + 1) * half].rearrange("n p r -> p n r"),
                             fin[:, c * 2 * half * T:(c * 2 + 1) * half * T].rearrange("p (n r) -> p n r", r=T)
                             ).then_inc(s_out, 16)
            sp.wait_ge(s_out, 32)
            sp.wait_ge(s_acc0, 32)
            sp.wait_ge(s_init, 16)

        @block.tensor
        def _(pe):
            def sumsq(b):
                pe.wait_ge(s_sq, b + 1)
                if b >= 1:
                    pe.wait_ge(s_guard, b)
                if b >= 4:
                    pe.wait_ge(s_ex, b - 3)
                pe.matmul(ss_ps, head_block, sq[:, b % 2, :], start=True, stop=True).then_inc(s_ss, 1)

            def turn_v(b):
                if b >= 4:
                    pe.wait_ge(s_zT, b - 3)
                elif b >= 1:
                    pe.wait_ge(s_vm, 2 * b)
                for c in range(KC):
                    last = pe.transpose(t_ps[:, c, :], qc[:, b, 1, c * P:(c + 1) * P], ident)
                last.then_inc(s_vT, 1)

            def scores(b, i):
                n = b * PAIRS + i
                if i == 0:
                    pe.wait_ge(s_qeo, 2 * (b + 1))
                    pe.wait_ge(s_kn, b + 1)
                if n >= 2:
                    pe.wait_ge(s_p, n - 1)
                q = 32 * i
                for c in range(KC):
                    last = pe.matmul(score_ps[:, i % 2, c, :], kn[q:q + 32, b % 2, c * P:(c + 1) * P],
                                     qeo[q:q + 32, b % 2, :, :].rearrange("p a n -> p (a n)"), start=True, stop=True,
                                     tile_position=(q, 0))
                last.then_inc(s_sc, 1)

            def pv(b, step):
                if step == 0:
                    pe.wait_ge(s_p, PAIRS * (b + 1))
                    pe.wait_ge(s_vm, 2 * (b + 1))
                    if b >= 1:
                        pe.wait_ge(s_att, b)
                        pe.wait_ge(s_lnden, b)
                parity, c = step // 2, step % 2
                for acc, den in ((num_ps, False), (den_ps, True)):
                    for i in range(PAIRS):
                        q = 32 * i
                        w = ones_half[parity] if den else vm[:, b % 3, parity, c, q:q + 32]
                        last = pe.matmul(acc[q:q + 32, :], w, probs[:, b % 2, i, c, parity * T:(parity + 1) * T],
                                         start=step == 0, stop=step == 3)
                if step == 3:
                    last.then_inc(s_pv, 1)

            def turn_z(b):
                pe.wait_ge(s_z, b + 1)
                pe.wait_ge(s_vm, 2 * min(b + 4, B))
                if b >= 1:
                    pe.wait_ge(s_zT, b)
                for c in range(KC):
                    last = pe.transpose(t_ps[:, c, :], rows[:, b, c * P:(c + 1) * P], ident)
                last.then_inc(s_zps, 1)

            def logits(b):
                pe.wait_ge(s_zT, b + 1)
                pe.wait_ge(s_guard, min(b + 4, B))
                if b >= 1:
                    pe.wait_ge(s_ex, b)
                    pe.wait_ge(s_prod, b)
                for c in range(KC):
                    last = pe.matmul(logit_ps, zT[:, b, c, :], wrT[:, c, :], start=c == 0, stop=c == KC - 1)
                last.then_inc(s_lg, 1)

            def positions(b):
                pe.wait_ge(s_ch, b + 1)
                pe.wait_ge(s_bef, b + 1)
                pe.wait_ge(s_guard, min(b + 5, B))
                pe.wait_ge(s_ex, b + 1)
                pe.matmul(pos_ps, tri[:, :], chosen[:, b, :], start=True, stop=False)
                pe.matmul(pos_ps, ones_bf[:, :], before[:, b, :], start=False, stop=True).then_inc(s_pos, 1)

            pe.wait_ge(s_cst, 16)
            sumsq(0)
            pe.wait_ge(s_in[0], 32)
            turn_v(0)
            pe.wait_ge(s_wr, 16)
            for c in range(KC):
                last = pe.transpose(bank[0][:, c * E:(c + 1) * E], wr_sb[:, c * P:(c + 1) * P], ident[0:E, 0:E])
            last.then_inc(s_wrps, 1)
            pe.wait_ge(s_wrT, 1)
            for t in range(B + 2):
                for i in range(PAIRS):
                    if t < B:
                        scores(t, i)
                    if 0 <= t - 1 < B:
                        pv(t - 1, i)
                    if i == 0 and t + 1 < B:
                        sumsq(t + 1)
                        pe.wait_ge(s_in[t + 1], 32)
                        turn_v(t + 1)
                    if i == 2 and t >= 3:
                        positions(t - 3)
                    if i == 1 and t >= 2:
                        turn_z(t - 2)
                    if i == 3 and t >= 2:
                        logits(t - 2)

            def sh_gate_up(b):
                pe.wait_ge(s_zT, b + 1)
                if b >= 2:
                    pe.wait_ge(s_h_s, b - 1)
                for k, w in enumerate((wsg, wsu)):
                    for c in range(KC):
                        last = pe.matmul(score_ps[:, b % 2, k, 0:FS], zT[:, b, c, :], w[:, c, :],
                                         start=c == 0, stop=c == KC - 1)
                last.then_inc(s_shps, 1)

            def sh_turn(b):
                pe.wait_ge(s_h_s, b + 1)
                if b >= 2:
                    pe.wait_ge(s_hT_s, b - 1)
                for c, (f0, n) in enumerate(FS_CHUNKS):
                    last = pe.transpose(bank[4 + b % 2][0:n, c * P:(c + 1) * P], hs[:, b % 2, f0:f0 + n], ident)
                last.then_inc(s_hps_s, 1)

            def sh_down(b):
                pe.wait_ge(s_hT_s, b + 1)
                if b >= 1:
                    pe.wait_ge(s_base, b)
                for c, (f0, n) in enumerate(FS_CHUNKS):
                    last = pe.matmul(bank[6][:, 0:T], hsT[0:n, b % 2, c, :], wsd[0:n, c, :], start=c == 0, stop=c == 2)
                last.then_inc(s_y_s, 1)

            pe.wait_ge(s_wsh, 80)
            pe.wait_ge(s_p, PAIRS * B)
            pe.wait_ge(s_lnden, B)
            pe.wait_ge(s_att, B)
            for b in range(B + 2):
                if b < B:
                    sh_gate_up(b)
                if b == 1:
                    positions(B - 1)
                    pe.wait_ge(s_bef, B + 1)
                    pe.wait_ge(s_prod, B)
                    pe.matmul(pos_ps, ones_bf[:, :], before[:, B, :], start=True, stop=True).then_inc(s_cnt, 1)
                if 1 <= b <= B:
                    sh_turn(b - 1)
                if b >= 2:
                    sh_down(b - 2)

            def turn_slots(e, r, par):
                pe.wait_ge(s_x_in[r], e // RING * 16 + 16 if isinstance(e, int) else (e - r) * (16 // RING) + 16)
                if not (isinstance(e, int) and e < 2):
                    pe.wait_ge(s_xT, e - 1)
                for t in range(TILES):
                    for c in range(KC):
                        k = t * KC + c
                        last = pe.transpose(bank[par][:, k * P:(k + 1) * P], slot[:, r, t, c * P:(c + 1) * P], ident)
                last.then_inc(s_xps, 1)

            def gate_up(e, r, par, t):
                if t == 0:
                    pe.wait_ge(s_w_in[r], e // RING * 48 + 48 if isinstance(e, int) else (e - r) * (48 // RING) + 48)
                    pe.wait_ge(s_xT, e + 1)
                if not (isinstance(e, int) and e == 0):
                    pe.wait_ge(s_h[t], e)
                for c in range(KC):
                    last = pe.matmul(bank[2 + t][:, 0:2 * F], slotT[:, par, t, c, :], wgu[:, r, c, :],
                                     start=c == 0, stop=c == KC - 1)
                last.then_inc(s_gu[t], 1)

            def turn_hidden(e, t):
                pe.wait_ge(s_h[t], e + 1)
                if not (isinstance(e, int) and e == 0):
                    pe.wait_ge(s_hT[t], e)
                for c in range(2):
                    last = pe.transpose(bank[4 + t][0:FH, c * P:(c + 1) * P], h[:, t, c * FH:(c + 1) * FH], ident)
                last.then_inc(s_hps[t], 1)

            def down(e, r, t):
                pe.wait_ge(s_hT[t], e + 1)
                if not (isinstance(e, int) and e == 0):
                    pe.wait_ge(s_ys[t], e)
                for c in range(2):
                    last = pe.matmul(bank[6 + t][:, 0:T], hT[:, t, c, :], wd[:, r, c, :], start=c == 0, stop=c == 1)
                last.then_inc(s_y[t], 1)

            pe.wait_ge(s_h_s, B)
            pe.wait_ge(s_hT_s, B)
            pe.wait_ge(s_base, B)
            pe.wait_ge(s_cmax, 1)
            turn_slots(0, 0, 0)

            def expert(e, r):
                first, final = isinstance(e, int) and e == 0, isinstance(e, int) and e == E - 1
                if not final:
                    turn_slots(e + 1, (r + 1) % RING, (r + 1) % 2)
                gate_up(e, r, r % 2, 0)
                if not first:
                    turn_hidden(e - 1, 1)
                    down(e - 1, (r - 1) % RING, 0)
                gate_up(e, r, r % 2, 1)
                turn_hidden(e, 0)
                if not first:
                    down(e - 1, (r - 1) % RING, 1)

            experts(pe, expert)
            turn_hidden(E - 1, 1)
            down(E - 1, (E - 1) % RING, 0)
            down(E - 1, (E - 1) % RING, 1)

            pe.wait_ge(s_flag, 1)
            n_max = pe.value_load(flag[0:1, 0:1], min_val=0, max_val=TOKENS)
            with pe.If(n_max > TILES * P):
                for t in range(TILES):
                    pe.wait_ge(s_ys[t], E)
                with pe.Fori(0, E) as e:
                    pe.wait_ge(o_in, e * 64 + 64)
                    for c in range(KC):
                        last = pe.transpose(bank[0][:, c * P:(c + 1) * P], slot[:, 0, 0, c * P:(c + 1) * P], ident)
                    last.then_inc(o_xps, 1)
                    pe.wait_ge(o_xT, e + 1)
                    for c in range(KC):
                        last = pe.matmul(bank[2][:, 0:2 * F], slotT[:, 0, 0, c, :], wgu[:, 0, c, :],
                                         start=c == 0, stop=c == KC - 1)
                    last.then_inc(o_gu, 1)
                    pe.wait_ge(o_h, e + 1)
                    for c in range(2):
                        last = pe.transpose(bank[4][0:FH, c * P:(c + 1) * P], h[:, 0, c * FH:(c + 1) * FH], ident)
                    last.then_inc(o_hps, 1)
                    pe.wait_ge(o_hT, e + 1)
                    for c in range(2):
                        last = pe.matmul(bank[6][:, 0:T], hT[:, 0, c, :], wd[:, 0, c, :], start=c == 0, stop=c == 1)
                    last.then_inc(o_y, 1)

        @block.scalar
        def _(act):
            def inv_norms(b):
                act.wait_ge(s_guard, b + 1)
                act.activation(lns[:, b % 2, :], ssg[:, b % 2, :], ACT.Ln, scale=SHIFT).then_inc(s_lnss, 1)
                act.wait_ge(s_lnss, b + 1)
                if b >= 2:
                    act.wait_ge(s_qeo, 2 * (b - 1))
                    act.wait_ge(s_kn, b - 1)
                act.activation(rnorm[:, b % 2, :], lns[:, b % 2, :], ACT.Exp, scale=-0.5).then_inc(s_rn, 1)

            def copy_v(b):
                act.wait_ge(s_vT, b + 1)
                if b >= 3:
                    act.wait_ge(s_pv, b - 2)
                for parity in range(2):
                    heads = "p c (i a d) -> p c i a d"
                    src = t_ps.rearrange(heads, i=PAIRS, a=2)[:, :, :, parity, :]
                    dst = vm[:, b % 3, parity, :, :].rearrange(heads, i=PAIRS, a=2)[:, :, :, parity, :]
                    act.copy(dst, src).then_inc(s_vm, 1)

            def exp_scores(b, i):
                act.wait_ge(s_sc, b * PAIRS + i + 1)
                if b >= 2 and i == 0:
                    act.wait_ge(s_pv, b - 1)
                act.activation(probs[:, b % 2, i, :, :], score_ps[:, i % 2, :, :], ACT.Exp,
                               scale=ALPHA * UNSHIFT).then_inc(s_p, 1)

            def inv_den(b):
                act.wait_ge(s_pv, b + 1)
                act.activation(lnden[:, b % 2, :], den_ps, ACT.Ln).then_inc(s_lnden, 1)
                act.wait_ge(s_lnden, b + 1)
                if b >= 2:
                    act.wait_ge(s_att, b - 1)
                act.activation(rden[:, b % 2, :], lnden[:, b % 2, :], ACT.Exp, scale=-1.0).then_inc(s_rden, 1)

            def copy_zT(b):
                act.wait_ge(s_zps, b + 1)
                act.copy(zT[:, b, :, :], t_ps).then_inc(s_zT, 1)

            def exp_logits(b):
                act.wait_ge(s_lg, b + 1)
                act.wait_ge(s_negm, b + 1)
                act.activation(ex[:, b, :], logit_ps, ACT.Exp, bias=negm[:, b:b + 1],
                               accum_out=esum[:, b:b + 1]).then_inc(s_ex, 1)

            act.wait_ge(s_gate, 32)
            act.activation(tg[:, :], gates[:, :], ACT.Tanh).then_inc(s_tg, 1)
            act.preload_act_table_set("natural_log_exp_and_others")
            act.wait_ge(s_setup, 3)
            inv_norms(0)
            copy_v(0)
            act.wait_ge(s_wrps, 1)
            act.copy(wrT[:, :, :].rearrange("p c e -> p (c e)"), bank[0][:, 0:KC * E]).then_inc(s_wrT, 1)
            for t in range(B + 2):
                if t >= 2:
                    inv_den(t - 2)
                for i in range(PAIRS):
                    if t < B:
                        exp_scores(t, i)
                    if i == 0 and t + 1 < B:
                        inv_norms(t + 1)
                    if i == 1 and t + 1 < B:
                        copy_v(t + 1)
                    if i == 1 and t >= 2:
                        copy_zT(t - 2)
                if t >= 2:
                    exp_logits(t - 2)

            for b in range(B + 1):
                if b < B:
                    act.wait_ge(s_shps, b + 1)
                    if b >= 2:
                        act.wait_ge(s_h_s, b - 1)
                    act.activation(sgs[:, b % 2, :], score_ps[:, b % 2, 0, 0:FS], ACT.Silu).then_inc(s_sg_s, 1)
                if b >= 1:
                    act.wait_ge(s_hps_s, b)
                    if b >= 3:
                        act.wait_ge(s_y_s, b - 2)
                    k = (b - 1) % 2
                    act.copy(hsT[:, k, 0:2, :], bank[4 + k][:, 0:2 * P].rearrange("p (c n) -> p c n", c=2))
                    act.copy(hsT[0:96, k, 2, :], bank[4 + k][0:96, 2 * P:3 * P]).then_inc(s_hT_s, 1)

            def silu(e, t):
                act.wait_ge(s_gu[t], e + 1)
                if not (isinstance(e, int) and e == 0):
                    act.wait_ge(s_h[t], e)
                act.activation(sg[:, t, :], bank[2 + t][:, 0:F], ACT.Silu).then_inc(s_sg[t], 1)

            def copy_hidden(e, t):
                act.wait_ge(s_hps[t], e + 1)
                if not (isinstance(e, int) and e == 0):
                    act.wait_ge(s_y[t], e)
                act.copy(hT[:, t, :, :], bank[4 + t][0:FH, 0:2 * P].rearrange("p (c n) -> p c n", c=2)).then_inc(s_hT[t], 1)

            def scale_y(e, r, t):
                act.wait_ge(s_y[t], e + 1)
                act.wait_ge(s_wcol, e + 1)
                act.activation(ysc[:, r, t, :], bank[6 + t][:, 0:T], ACT.Copy,
                               scale=wcol[:, r, t:t + 1]).then_inc(s_ys[t], 1)

            def expert(e, r):
                first = isinstance(e, int) and e == 0
                silu(e, 0)
                if not first:
                    copy_hidden(e - 1, 1)
                    scale_y(e - 1, (r - 1) % RING, 0)
                silu(e, 1)
                copy_hidden(e, 0)
                if not first:
                    scale_y(e - 1, (r - 1) % RING, 1)

            experts(act, expert)
            copy_hidden(E - 1, 1)
            for t in range(TILES):
                scale_y(E - 1, (E - 1) % RING, t)

            act.wait_ge(s_flag, 1)
            n_max = act.value_load(flag[0:1, 0:1], min_val=0, max_val=TOKENS)
            with act.If(n_max > TILES * P):
                with act.Fori(0, E) as e:
                    act.wait_ge(o_gu, e + 1)
                    act.activation(sg[:, 0, :], bank[2][:, 0:F], ACT.Silu).then_inc(o_sg, 1)
                    act.wait_ge(o_hps, e + 1)
                    act.copy(hT[:, 0, :, :], bank[4][0:FH, 0:2 * P].rearrange("p (c n) -> p c n", c=2)).then_inc(o_hT, 1)
                    act.wait_ge(o_y, e + 1)
                    act.wait_ge(o_wcol, e + 1)
                    act.activation(ysc[:, 0, 0, :], bank[6][:, 0:T], ACT.Copy, scale=wcol[:, 0, 0:1]).then_inc(o_ys, 1)

        @block.vector
        def _(dve):
            def ln1_stats(b):
                dve.wait_ge(s_in[b], 32)
                dve.bn_stats(st1[:, b, :], xs[:, b, :]).then_inc(s_st1, 1)
                dve.wait_ge(s_st1, b + 1)
                dve.bn_aggr(mv1[:, b, :], st1[:, b, :]).then_inc(s_mv1, 1)

            def q_and_squares(b):
                dve.wait_ge(s_rstd1, b + 1)
                dve.tensor_scalar(qc[:, b, 0, :], xs[:, b, :], mv1[:, b, 0:1], rstd1[:, b:b + 1],
                                  ALU.subtract, ALU.mult).then_inc(s_q, 1)
                dve.wait_ge(s_q, b + 1)
                if b >= 2:
                    dve.wait_ge(s_ss, b - 1)
                qcb = qc[:, b, :, :].rearrange("p a n -> p (a n)")
                dve.tensor_tensor(sq[:, b % 2, :], qcb, qcb, ALU.mult).then_inc(s_sq, 1)

            def guard(b):
                dve.wait_ge(s_ss, b + 1)
                if b >= 2:
                    dve.wait_ge(s_lnss, b - 1)
                dve.tensor_scalar(ssg[:, b % 2, :], ss_ps, NORM_EPS_SQ, None, ALU.max).then_inc(s_guard, 1)

            def mask_q(b):
                dve.wait_ge(s_rn, b + 1)
                if b >= 2:
                    dve.wait_ge(s_sc, PAIRS * (b - 1))
                for parity, mask in enumerate((even_mask, odd_mask)):
                    dve.scalar_tensor_tensor(out=qeo[:, b % 2, parity, :], in0=qc[:, b, 0, :], scalar=mask,
                                             in1=rnorm[:, b % 2, 0:T], op0=ALU.mult, op1=ALU.mult).then_inc(s_qeo, 1)

            def residual(b):
                dve.wait_ge(s_rden, b + 1)
                if b >= 2:
                    dve.wait_ge(s_x2, b - 1)
                dve.tensor_tensor(att[:, b % 2, :], num_ps, rden[:, b % 2, :], ALU.mult).then_inc(s_att, 1)
                dve.wait_ge(s_att, b + 1)
                dve.scalar_tensor_tensor(out=x2[:, b, :], in0=att[:, b % 2, :], scalar=tg[:, 0:1], in1=xs[:, b, :],
                                         op0=ALU.mult, op1=ALU.add).then_inc(s_x2, 1)
                dve.wait_ge(s_x2, b + 1)
                dve.bn_stats(st2[:, b, :], x2[:, b, :]).then_inc(s_st2, 1)
                dve.wait_ge(s_st2, b + 1)
                dve.bn_aggr(mv2[:, b, :], st2[:, b, :]).then_inc(s_mv2, 1)

            def ln2(b):
                dve.wait_ge(s_rstd2, b + 1)
                dve.tensor_scalar(rows[:, b, 0:T], x2[:, b, :], mv2[:, b, 0:1], rstd2[:, b:b + 1],
                                  ALU.subtract, ALU.mult).then_inc(s_z, 1)

            def top_logit(b):
                dve.wait_ge(s_lg, b + 1)
                dve.max(m8[:, b, :], logit_ps).then_inc(s_m8, 1)
                dve.wait_ge(s_m8, b + 1)
                dve.tensor_scalar(negm[:, b:b + 1], m8[:, b, 0:1], -1.0, None, ALU.mult).then_inc(s_negm, 1)

            def choose(b):
                dve.wait_ge(s_ex, b + 1)
                dve.reciprocal(rsum[:, b:b + 1], esum[:, b:b + 1]).then_inc(s_rsum, 1)
                dve.wait_ge(s_rsum, b + 1)
                dve.tensor_scalar(score[:, b, :], ex[:, b, :], rsum[:, b:b + 1], None, ALU.mult).then_inc(s_score, 1)
                dve.wait_ge(s_score, b + 1)
                dve.max(v8[:, b, :], score[:, b, :]).then_inc(s_v8, 1)
                dve.wait_ge(s_v8, b + 1)
                dve.max_index(idx8[:, b, :], v8[:, b, :], score[:, b, :]).then_inc(s_idx, 1)
                dve.tensor_reduce(wsum[:, b:b + 1], v8[:, b, 0:TOPK], AX.X, ALU.add).then_inc(s_wsum, 1)
                dve.wait_ge(s_idx, b + 1)
                dve.tensor_copy(idxf[:, b, :], idx8[:, b, 0:TOPK]).then_inc(s_idxf, 1)
                dve.wait_ge(s_wsum, b + 1)
                dve.tensor_scalar(wsum[:, b:b + 1], wsum[:, b:b + 1], 1e-20, None, ALU.add).then_inc(s_weps, 1)
                dve.wait_ge(s_idxf, b + 1)
                if b >= 2:
                    dve.wait_ge(s_prod, b - 1)
                dve.tensor_tensor(onehot[:, b % 2, :, :], iota_e.unsqueeze(1).to_broadcast([P, TOPK, E]),
                                  idxf[:, b, :].unsqueeze(2).to_broadcast([P, TOPK, E]), ALU.is_equal).then_inc(s_oh, 1)
                dve.wait_ge(s_weps, b + 1)
                dve.reciprocal(wrec[:, b:b + 1], wsum[:, b:b + 1]).then_inc(s_wrec, 1)
                dve.wait_ge(s_oh, b + 1)
                with nc.allow_low_precision(reason="sums of ones and zeros, at most 1"):
                    dve.tensor_reduce(chosen[:, b, :], onehot[:, b % 2, :, :].rearrange("p k e -> p e k"),
                                      AX.X, ALU.add).then_inc(s_ch, 1)
                dve.wait_ge(s_wrec, b + 1)
                dve.tensor_scalar(wgate[:, b:b + 1], wrec[:, b:b + 1], tg[:, 1:2], None, ALU.mult).then_inc(s_wg, 1)
                dve.wait_ge(s_ch, b + 1)
                dve.wait_ge(s_wg, b + 1)
                dve.scalar_tensor_tensor(out=rows[:, b, W_AT:W_AT + E], in0=score[:, b, :], scalar=wgate[:, b:b + 1],
                                         in1=chosen[:, b, :], op0=ALU.mult, op1=ALU.mult).then_inc(s_w, 1)

            def destinations(b):
                dve.wait_ge(s_pos, b + 1)
                if b >= 2:
                    dve.wait_ge(s_posk, b - 1)
                dve.tensor_tensor(prod[:, b % 2, :, :], onehot[:, b % 2, :, :],
                                  pos_ps.unsqueeze(1).to_broadcast([P, TOPK, E]), ALU.mult).then_inc(s_prod, 1)
                dve.wait_ge(s_prod, b + 1)
                dve.tensor_reduce(posk[:, b, :], prod[:, b % 2, :, :], AX.X, ALU.add).then_inc(s_posk, 1)
                dve.wait_ge(s_posk, b + 1)
                dve.tensor_scalar(over[:, b, :], posk[:, b, :], float(CAP), float(E * CAP), ALU.is_ge, ALU.mult).then_inc(s_over, 1)
                dve.scalar_tensor_tensor(out=dest_f[:, b, :], in0=idxf[:, b, :], scalar=float(CAP), in1=posk[:, b, :],
                                         op0=ALU.mult, op1=ALU.add).then_inc(s_d1, 1)
                dve.wait_ge(s_over, b + 1)
                dve.wait_ge(s_d1, b + 1)
                dve.tensor_tensor(dest[:, b, :], dest_f[:, b, :], over[:, b, :], ALU.add).then_inc(s_dest, 1)

            dve.memset(vm[:, :, :, :, :], 0.0).then_inc(s_setup, 1)
            dve.memset(ones_bf[:, :], 1.0).then_inc(s_setup, 1)
            dve.wait_ge(s_cst, 16)
            dve.tensor_copy(tri[:, :], cst[:, C_TRI:C_TRI + P]).then_inc(s_setup, 1)
            ln1_stats(0)
            q_and_squares(0)
            ln1_stats(1)
            guard(0)
            q_and_squares(1)
            mask_q(0)
            dve.wait_ge(s_tg, 1)
            for t in range(B + 3):
                if 0 <= t - 2 < B:
                    residual(t - 2)
                if t + 1 < B:
                    guard(t + 1)
                if t + 2 < B:
                    ln1_stats(t + 2)
                if 0 <= t - 2 < B:
                    ln2(t - 2)
                if t >= 3:
                    destinations(t - 3)
                if t + 1 < B:
                    mask_q(t + 1)
                if 0 <= t - 2 < B:
                    top_logit(t - 2)
                if t + 2 < B:
                    q_and_squares(t + 2)
                if 0 <= t - 2 < B:
                    choose(t - 2)
            dve.wait_ge(s_cnt, 1)
            dve.tensor_reduce(cmax[:, :], pos_ps, AX.X, ALU.max).then_inc(s_cmax, 1)
            dve.wait_ge(s_cmax, 1)
            dve.tensor_copy(flag[:, :], cmax[:, :]).then_inc(s_flag, 1)

            for b in range(B + 2):
                if b < B:
                    dve.wait_ge(s_sg_s, b + 1)
                    if b >= 2:
                        dve.wait_ge(s_hps_s, b - 1)
                    dve.tensor_tensor(hs[:, b % 2, :], score_ps[:, b % 2, 1, 0:FS], sgs[:, b % 2, :], ALU.mult).then_inc(s_h_s, 1)
                if b >= 2:
                    dve.wait_ge(s_y_s, b - 1)
                    if b >= 4:
                        dve.wait_ge(s_seed[b % 2], 16 * ((b - 4) // 2 + 1))
                    dve.scalar_tensor_tensor(out=base[:, b % 2, :], in0=bank[6][:, 0:T], scalar=tg[:, 1:2],
                                             in1=x2[:, b - 2, :], op0=ALU.mult, op1=ALU.add).then_inc(s_base, 1)

            def copy_slots(e, par):
                dve.wait_ge(s_xps, e + 1)
                if not (isinstance(e, int) and e < 2):
                    dve.wait_ge(s_gu[TILES - 1], e - 1)
                dve.tensor_copy(slotT[:, par, :, :, :].rearrange("p t c n -> p (t c n)"), bank[par]).then_inc(s_xT, 1)

            def hidden(e, t):
                dve.wait_ge(s_sg[t], e + 1)
                if not (isinstance(e, int) and e == 0):
                    dve.wait_ge(s_hps[t], e)
                dve.tensor_tensor(h[:, t, :], bank[2 + t][:, F:2 * F], sg[:, t, :], ALU.mult).then_inc(s_h[t], 1)

            copy_slots(0, 0)

            def expert(e, r):
                if not (isinstance(e, int) and e == E - 1):
                    copy_slots(e + 1, (r + 1) % 2)
                for t in range(TILES):
                    hidden(e, t)

            experts(dve, expert)

            dve.wait_ge(s_flag, 1)
            n_max = dve.value_load(flag[0:1, 0:1], min_val=0, max_val=TOKENS)
            with dve.If(n_max > TILES * P):
                with dve.Fori(0, E) as e:
                    dve.wait_ge(o_xps, e + 1)
                    dve.tensor_copy(slotT[:, 0, 0, :, :].rearrange("p c n -> p (c n)"), bank[0][:, 0:T]).then_inc(o_xT, 1)
                    dve.wait_ge(o_sg, e + 1)
                    dve.tensor_tensor(h[:, 0, :], bank[2][:, F:2 * F], sg[:, 0, :], ALU.mult).then_inc(o_h, 1)
            fin = probs[:, :, :, :, :].rearrange("p a b c d -> p (a b c d)")
            n = B // 2 * T
            for c in range(2):
                dve.wait_ge(s_fin_in, 64)
                dve.tensor_tensor(fin[:, c * 2 * n:(c * 2 + 1) * n], fin[:, c * 2 * n:(c * 2 + 1) * n],
                                  fin[:, (c * 2 + 1) * n:(c * 2 + 2) * n], ALU.add).then_inc(s_fin, 1)

        @block.gpsimd
        def _(pool):
            pool.memset(row0[:, :], 0.0).then_inc(s_row0, 1)
            pool.wait_ge(s_row0, 1)
            pool.iota(row0[:, TOK_AT:TOK_AT + 1].bitcast(I32), pattern=[[0, 1]], base=TOKENS, channel_multiplier=1).then_inc(s_row0, 1)
            pool.iota(rows[:, :, TOK_AT:TOK_AT + 1].bitcast(I32), pattern=[[P, B], [0, 1]], base=0, channel_multiplier=1).then_inc(s_pconst, 1)
            pool.memset(before[:, 0, :], 0.0).then_inc(s_bef, 1)
            pool.wait_ge(s_cst, 16)
            pool.wait_ge(s_pconst, 1)

            def rstd(b, s_mv, mv, s_ve, ve, s_rs, rs):
                pool.wait_ge(s_mv, b + 1)
                pool.tensor_scalar(ve[:, b:b + 1], mv[:, b, 1:2], LN_EPS, None, ALU.add).then_inc(s_ve, 1)
                pool.wait_ge(s_ve, b + 1)
                pool.tensor_tensor(rs[:, b:b + 1], ve[:, b:b + 1], minus_half, ALU.pow).then_inc(s_rs, 1)

            def norm_k(b):
                pool.wait_ge(s_rn, b + 1)
                pool.wait_ge(s_in[b], 32)
                if b >= 2:
                    pool.wait_ge(s_sc, PAIRS * (b - 1))
                pool.tensor_tensor(kn[:, b % 2, :], qc[:, b, 1, :], rnorm[:, b % 2, T:2 * T], ALU.mult).then_inc(s_kn, 1)

            def scatter(b):
                pool.wait_ge(s_dest, b + 1)
                pool.wait_ge(s_w, b + 1)
                pool.wait_ge(s_z, b + 1)
                if b == 0:
                    pool.wait_ge(s_init, 16)
                for k in range(TOPK):
                    pool.indirect_dma_start(
                        out=slots_dram[:, :], out_offset=bass.IndirectOffsetOnAxis(ap=dest[:, b, k:k + 1], axis=0),
                        in_=rows[:, b, :], in_offset=None, bounds_check=E * CAP - 1, oob_is_err=False).then_inc(s_scat, 16)

            def count(b):
                pool.wait_ge(s_ch, b + 1)
                pool.wait_ge(s_bef, b + 1)
                pool.tensor_tensor(before[:, b + 1, :], before[:, b, :], chosen[:, b, :], ALU.add).then_inc(s_bef, 1)

            ln1 = (s_mv1, mv1, s_ve1, ve1, s_rstd1, rstd1)
            ln2 = (s_mv2, mv2, s_ve2, ve2, s_rstd2, rstd2)
            rstd(0, *ln1)
            rstd(1, *ln1)
            norm_k(0)
            for t in range(B + 3):
                if 0 <= t - 2 < B:
                    rstd(t - 2, *ln2)
                if t + 2 < B:
                    rstd(t + 2, *ln1)
                if t + 1 < B:
                    norm_k(t + 1)
                if t >= 3:
                    scatter(t - 3)
                if 0 <= t - 2 < B:
                    count(t - 2)

            def slot_weights(e, r):
                pool.wait_ge(s_x_in[r], e // RING * 16 + 16 if isinstance(e, int) else (e - r) * (16 // RING) + 16)
                w = slot[:, r, :, W_AT + e:W_AT + e + 1] if isinstance(e, int) else slot[:, r, :, bass.ds(e + W_AT, 1)]
                pool.tensor_copy(wcol[:, r, :].unsqueeze(2), w).then_inc(s_wcol, 1)

            def add_rows(e, r, t):
                pool.wait_ge(s_ys[t], e + 1)
                if not (isinstance(e, int) and e == 0):
                    pool.wait_ge(s_acc[t], e * 16)
                pool.sem_inc(s_go, 1)
                pool.indirect_dma_start(
                    out=acc_dram[t][:, :],
                    out_offset=bass.IndirectOffsetOnAxis(ap=slot[:, r, t, TOK_AT:TOK_AT + 1].bitcast(U32), axis=0),
                    in_=ysc[:, r, t, :], in_offset=None, compute_op=ALU.add).then_inc(s_acc[t], 16)

            pool.wait_ge(s_acc0, 32)
            for i in range(2):
                pool.wait_ge(s_seed[i], 16 * B // 2)

            def expert(e, r):
                slot_weights(e, r)
                if not (isinstance(e, int) and e == 0):
                    for t in range(TILES):
                        add_rows(e - 1, (r - 1) % RING, t)

            experts(pool, expert)
            for t in range(TILES):
                add_rows(E - 1, (E - 1) % RING, t)

            pool.wait_ge(s_flag, 1)
            n_max = pool.value_load(flag[0:1, 0:1], min_val=0, max_val=TOKENS)
            with pool.If(n_max > TILES * P):
                for t in range(TILES):
                    pool.wait_ge(s_acc[t], 16 * E)
                pool.sem_inc(o_free, 1)
                with pool.Fori(0, E) as e:
                    pool.wait_ge(o_in, e * 64 + 64)
                    pool.tensor_copy(wcol[:, 0, 0:1], slot[:, 0, 0, bass.ds(e + W_AT, 1)]).then_inc(o_wcol, 1)
                    pool.wait_ge(o_ys, e + 1)
                    pool.sem_inc(s_go, 1)
                    pool.indirect_dma_start(
                        out=acc_dram[0][:, :],
                        out_offset=bass.IndirectOffsetOnAxis(ap=slot[:, 0, 0, TOK_AT:TOK_AT + 1].bitcast(U32), axis=0),
                        in_=ysc[:, 0, 0, :], in_offset=None, compute_op=ALU.add).then_inc(o_acc, 16)
                    pool.wait_ge(o_acc, e * 16 + 16)
                    pool.sem_inc(o_free, 1)


_INS = ['x', 'ctx_2048', 'g_xattn', 'g_ffn', 'L0_ffn_wg_router', 'L0_ffn_w_gate', 'L0_ffn_w_up', 'L0_ffn_w_down',
        'L0_ffn_ws_gate', 'L0_ffn_ws_up', 'L0_ffn_ws_down']
_OUTS = [((B, P, T), 'float32')]


def _constants():
    import numpy as np
    c = np.zeros((P, C_END), np.float32)
    p = np.arange(P)
    c[:, C_IDENT:C_IDENT + P] = np.eye(P)
    c[:, C_BLOCK:C_BLOCK + P] = p[:, None] // DH == p[None, :] // DH
    c[:, C_TRI:C_TRI + P] = p[:, None] < p[None, :]
    c[:, C_IOTA:C_IOTA + E] = np.arange(E)
    c[:, C_EVEN] = (p // DH % 2 == 0) * UNSHIFT
    c[:, C_ODD] = (p // DH % 2 == 1) * UNSHIFT
    c[:, C_ONES_E:C_ONES_E + DH] = 1
    c[:, C_ONES_O + DH:C_ONES_O + 2 * DH] = 1
    c[:, C_HALF] = -0.5
    return c


def kernel(**inputs):
    import numpy as _np
    import concourse.bacc as _bacc
    from concourse import mybir as _mybir
    from concourse.bass_utils import run_bass_kernel_spmd as _run

    nc = _bacc.Bacc("TRN2", target_bir_lowering=False, num_devices=1)
    arrays, args = {}, []
    for name in _INS:
        a = _np.ascontiguousarray(inputs[name])
        arrays[f"in_{name}_dram"] = a
        args.append(nc.dram_tensor(f"in_{name}_dram", a.shape, _mybir.dt.from_np(a.dtype), kind="ExternalInput").ap())
    arrays["consts_dram"] = _constants()
    args.append(nc.dram_tensor("consts_dram", arrays["consts_dram"].shape, _mybir.dt.float32, kind="ExternalInput").ap())
    for i, (shape, dtype) in enumerate(_OUTS):
        args.append(nc.dram_tensor(f"out_{i}_dram", shape, _mybir.dt.from_np(_np.dtype(dtype)), kind="ExternalOutput").ap())
    flamingo_block_kernel(nc, *args)
    r = _run(nc, [arrays], core_ids=[0])
    return r.results[0]["out_0_dram"]
```

```python
import concourse.bass as bass
from concourse import mybir
from contextlib import ExitStack

F32 = mybir.dt.float32
F32R = mybir.dt.float32r
BF16 = mybir.dt.bfloat16
U32 = mybir.dt.uint32
I32 = mybir.dt.int32
ALU = mybir.AluOpType
ACT = mybir.ActivationFunctionType
AX = mybir.AxisListType

P = 128
B, T = 8, 256
NH, DH = 8, 16
PAIRS = 4
KC = 2
E, F, TOPK = 32, 176, 6
FH = F // 2
FS = 2 * F
FS_CHUNKS = [(0, 128), (128, 128), (256, 96)]
TOKENS = B * P
CAP = 2 * (TOKENS * TOPK // E)
TILES = 2
ALPHA, LN_EPS = 5.0, 1e-5
NORM_EPS = 1e-12
SHIFT, UNSHIFT, LN_FLOOR = 2.0 ** 30, 2.0 ** 15, 2.0 ** -62
TCAP = CAP // P
SLOT = 8
QC = 4
RING = 4
FIN_CHUNKS = 4
LIST_STEP = 5

C_IDENT, C_BLOCK, C_TRI, C_IOTA, C_ONES_E, C_ONES_O, C_FLOOR, C_TOKEN, C_SMALL = (
    0, 128, 256, 384, 512, 544, 576, 577, 585)
SELK_W, SELQ_W = P + DH, P + 2 * DH
C_END = C_SMALL + PAIRS * (SELK_W + SELQ_W)


def flamingo_block_kernel(nc, x, ctx_kv, g_xattn, g_ffn, wg_router, w_gate, w_up, w_down,
                          ws_gate, ws_up, ws_down, consts, out):
    z_dram = nc.dram_tensor("z_rows", (TOKENS + P, T), F32, kind="Internal").ap()
    list_dram = nc.dram_tensor("slot_pairs", (E * CAP, SLOT), F32, kind="Internal").ap()
    acc_dram = [nc.dram_tensor(f"acc{i}", (TOKENS + P, T), F32, kind="Internal").ap() for i in range(TILES)]

    with ExitStack() as ctx:
        def sb(name, shape, dt=F32):
            return ctx.enter_context(nc.sbuf_tensor(name, shape, dt))

        def sem(name):
            return ctx.enter_context(nc.semaphore(name))

        cst = sb("cst", [P, C_SMALL])
        ident = cst[:, C_IDENT:C_IDENT + P]
        head_block = cst[:, C_BLOCK:C_BLOCK + P]
        iota, iota_e = cst[:, C_IOTA:C_IOTA + P], cst[:, C_IOTA:C_IOTA + E]
        ones_half = [cst[:, C_ONES_E:C_ONES_E + 32], cst[:, C_ONES_O:C_ONES_O + 32]]
        ln_floor = cst[:, C_FLOOR:C_FLOOR + 1]
        minus_half = sb("minus_half", [P, 1])[:, :]
        sel = sb("sel", [P, C_END - C_SMALL], F32R)
        tri = sb("tri", [P, P], BF16)
        ones_bf = sb("ones_bf", [P, P], BF16)
        gates = sb("gates", [P, 2])
        tg = sb("tg", [P, 2])
        wr_sb = sb("wr_sb", [E, T])
        wrT = sb("wrT", [P, KC, E])

        xs = sb("xs", [P, B, T])
        qc = sb("qc", [P, QC, 2, T])
        sq = sb("sq", [P, 2, 2 * T])
        rn = sb("rn", [P, 2, 2 * T])
        qkn = sb("qkn", [P, 2, 2 * T])
        hi_lo = sb("hi_lo", [P, 2, 2, 2 * T], F32R)
        hi, lo = hi_lo[:, 0, :, :], hi_lo[:, 1, :, :]
        stacks = sb("stacks", [P, 2 * PAIRS * 3 * T], F32R)
        kst = stacks[:, 0:2 * PAIRS * T].rearrange("p (b i n) -> p b i n", b=2, i=PAIRS)
        qst = stacks[:, 2 * PAIRS * T:6 * PAIRS * T].rearrange("p (b i a n) -> p b i a n", b=2, i=PAIRS, a=2)
        vm = sb("vm", [P, 3, 2, KC, P])
        probs = sb("probs", [P, 2, PAIRS, KC, 2 * T])
        lnden = sb("lnden", [P, 2, T])
        rden = sb("rden", [P, 2, T])
        att = sb("att", [P, 2, T])
        x2 = sb("x2", [P, B, T])
        st1, mv1 = sb("st1", [P, B, 6]), sb("mv1", [P, B, 2])
        st2, mv2 = sb("st2", [P, B, 6]), sb("mv2", [P, B, 2])
        ve1, rstd1 = sb("ve1", [P, B]), sb("rstd1", [P, B])
        ve2, rstd2 = sb("ve2", [P, B]), sb("rstd2", [P, B])
        z = sb("z", [P, B, T])
        pairs = sb("pairs", [P, B, TOPK, SLOT])
        zT = sb("zT", [P, B, KC, P])
        m8, negm, esum, rsum = sb("m8", [P, B, 8]), sb("negm", [P, B]), sb("esum", [P, B]), sb("rsum", [P, B])
        ex, score = sb("ex", [P, B, E]), sb("score", [P, B, E])
        v8, idx8, idxf = sb("v8", [P, B, 8]), sb("idx8", [P, B, 8], U32), sb("idxf", [P, B, TOPK])
        onehot = sb("onehot", [P, 2, TOPK, E])
        chosen = sb("chosen", [P, B, E], BF16)
        before = sb("before", [P, B, E], BF16)
        wsum, wrec, wgate = sb("wsum", [P, B]), sb("wrec", [P, B]), sb("wgate", [P, B])
        posk, over = sb("posk", [P, B, TOPK]), sb("over", [P, B, TOPK])
        prod = sb("prod", [P, 2, TOPK, E])
        dest_f = sb("dest_f", [P, B, TOPK])
        dest = sb("dest", [P, B, TOPK], U32)
        zero_row = sb("zero_row", [P, T])
        empty = sb("empty", [E * TCAP, P, SLOT])
        slot_tok, slot_w = sb("slot_tok", [P, E * TCAP], U32), sb("slot_w", [P, E * TCAP])
        cmax = sb("cmax", [P, 1])
        flag = sb("flag", [P, 1], I32)

        wsg, wsu = sb("wsg", [P, KC, FS]), sb("wsu", [P, KC, FS])
        wsd = sb("wsd", [P, 3, T])

        wgu = sb("wgu", [P, RING, KC, 2 * F])
        tok_g, tok_a = sb("tok_g", [P, RING, TILES], U32), sb("tok_a", [P, RING, TILES], U32)

        def carve(flat, at, *shape):
            n = 1
            for d in shape:
                n *= d
            dims = dict(zip("abcd", shape))
            order = " ".join(dims)
            return flat[:, at:at + n].rearrange(f"p ({order}) -> p {order}", **dims), at + n

        probs_flat = probs[:, :, :, :, :].rearrange("p a b c d -> p (a b c d)")
        sel_in = probs_flat[:, 0:C_END - C_SMALL]
        per = B // FIN_CHUNKS
        fin, _ = carve(probs_flat, 2 * RING * TILES * T, FIN_CHUNKS, TILES, per * T)
        ysc, at = carve(probs_flat, 0, RING, TILES, T)
        sgs, at = carve(probs_flat, at, 2, FS)
        hs, at = carve(probs_flat, at, 2, FS)
        sg, at = carve(probs_flat, at, TILES, F)
        h, at = carve(probs_flat, at, TILES, F)
        base, at = carve(probs_flat, at, 2, T)
        slot_list, _ = carve(probs_flat, at, P, SLOT)
        slot_list = slot_list[0:E * TCAP]
        slotT, hT = sgs[:, 0, 0:T], hs[0:FH, 0, 0:2 * P]
        slot, _ = carve(xs[:, :, :].rearrange("p b n -> p (b n)"), 0, RING, TILES, T)
        wd, _ = carve(qc[:, :, :, :].rearrange("p a b c -> p (a b c)"), 0, RING, 2, T)
        wd = wd[0:FH]
        slotT_hi, at = carve(stacks[:, :], 0, 2, TILES * KC * P)
        wgu_r, at = carve(stacks[:, :], at, 2, 2, KC, 2 * F)
        wd_at = at
        wd_r, _ = carve(stacks[:, :], at, 2, 2, 2, T)
        wd_r = wd_r[0:FH]
        hl_flat = hi_lo[:, :, :, :].rearrange("p a b n -> p (a b n)")
        slotT_lo, at = carve(hl_flat, 0, 2, TILES * KC * P)
        hT_r, _ = carve(hl_flat, at, TILES, 2, 2 * P)
        hT_r = hT_r[0:FH]
        wsgu_r, wsd_r = sb("wsgu_r", [P, 2, 2, KC, FS], F32R), sb("wsd_r", [P, 2, 3, T], F32R)
        hsT_r, _ = carve(stacks[:, :], wd_at, 2, 2, 3 * P)
        z_r, _ = carve(sel[:, :], 0, 2, 2, KC * P)
        score_ps = ctx.enter_context(nc.psum_tensor("score_ps", [P, 2, KC, 512], F32))
        bank = [score_ps[:, i // 2, i % 2, :] for i in range(4)]
        bank += [ctx.enter_context(nc.psum_tensor(f"bank{i}", [P, 512], F32))[:, :] for i in range(4, 8)]
        num_ps, den_ps, ss_ps = bank[4][:, 0:T], bank[4][:, T:2 * T], bank[6]
        t_ps = bank[7][:, 0:T].rearrange("p (c n) -> p c n", c=KC)
        logit_ps, pos_ps = bank[7][:, T:T + E], bank[6][:, 0:E]

        s_in = [sem(f"in_loaded{b}") for b in range(B)]
        s_cst, s_gate, s_wr, s_wsh = sem("consts_loaded"), sem("gates_loaded"), sem("router_loaded"), sem("shared_loaded")
        s_tg, s_setup, s_pconst, s_row0, s_wrps, s_wrT = (sem("tanh_gates"), sem("setup_dve"), sem("token_numbers"),
                                                  sem("empty_slots"), sem("router_turned"), sem("router_T"))
        s_zrow, s_init, s_acc0, s_zst = sem("zero_row"), sem("list_cleared"), sem("acc_zeroed"), sem("z_stored")
        s_list, s_lps, s_tok, s_tokg, s_toka = (sem("list_loaded"), sem("list_turned"), sem("slot_tokens"),
                                                sem("gather_tokens"), sem("add_tokens"))
        s_st1, s_mv1, s_ve1, s_rstd1 = sem("ln1_stats"), sem("ln1_mv"), sem("ln1_eps"), sem("ln1_rstd")
        s_q, s_sq, s_ss = sem("q_ln"), sem("squares"), sem("sumsq")
        s_lnss, s_rn, s_qkn, s_hi, s_lo = sem("ln_sumsq"), sem("rnorm"), sem("qk_normed"), sem("qk_hi"), sem("qk_lo")
        s_fills0, s_sel, s_zero, s_selc = sem("pool_constants"), sem("selections_loaded"), sem("zero_blocks"), sem("selections_cast")
        s_fill, s_stk_a, s_stk_d = sem("stacks_filled"), sem("stacks_copied_act"), sem("stacks_copied_dve")
        s_vT, s_vm = sem("v_turned"), sem("v_masked")
        s_sc, s_p, s_pv = sem("scores"), sem("probs"), sem("pv_done")
        s_lnden, s_rden, s_att, s_x2 = sem("ln_den"), sem("rden"), sem("att_normed"), sem("x2_ready")
        s_st2, s_mv2, s_ve2, s_rstd2, s_z = sem("ln2_stats"), sem("ln2_mv"), sem("ln2_eps"), sem("ln2_rstd"), sem("z_ready")
        s_zps, s_zT, s_lg = sem("z_turned"), sem("zT_ready"), sem("logits")
        s_m8, s_negm, s_ex, s_rsum, s_score = sem("max8"), sem("neg_max"), sem("exp_logits"), sem("rsum"), sem("router_score")
        s_v8, s_idx, s_idxf, s_oh, s_ch = sem("top8"), sem("top_idx"), sem("top_idx_f"), sem("onehot"), sem("chosen")
        s_wsum, s_weps, s_wrec, s_wg, s_w = sem("wsum"), sem("wsum_eps"), sem("wrec"), sem("wgate"), sem("row_weights")
        s_bef, s_pos, s_prod, s_posk = sem("before"), sem("positions"), sem("pos_prod"), sem("pos_k")
        s_over, s_d1, s_dest, s_scat = sem("over_cap"), sem("dest_raw"), sem("dest"), sem("scattered")
        s_cnt, s_cmax, s_flag = sem("counts"), sem("count_max"), sem("flag")
        s_shps, s_sg_s, s_h_s, s_hps_s, s_y_s, s_base = (
            sem("sh_gu"), sem("sh_silu"), sem("sh_h"), sem("sh_hturned"), sem("sh_down"), sem("sh_base"))
        s_wsh_hi, s_wsh_lo, s_zh, s_zl, s_hTh_s, s_hTl_s = (
            sem("shared_w_high"), sem("shared_w_low"), sem("z_high"), sem("z_low"), sem("sh_hT_high"), sem("sh_hT_low"))
        s_seed = [sem(f"sh_seeded{i}") for i in range(2)]
        s_w_in = [sem(f"expert_w_loaded{r}") for r in range(RING)]
        s_x_in = [sem(f"slots_gathered{r}") for r in range(RING)]
        s_xps, s_xh, s_xl = sem("slots_turned"), sem("slots_high"), sem("slots_low")
        s_gh, s_gl, s_dh, s_dl = sem("gate_up_w_high"), sem("gate_up_w_low"), sem("down_w_high"), sem("down_w_low")
        s_gu = [sem(f"gate_up{t}") for t in range(TILES)]
        s_sg = [sem(f"silu{t}") for t in range(TILES)]
        s_h = [sem(f"hidden{t}") for t in range(TILES)]
        s_hps = [sem(f"hidden_turned{t}") for t in range(TILES)]
        s_hTh = [sem(f"hidden_T_high{t}") for t in range(TILES)]
        s_hTl = [sem(f"hidden_T_low{t}") for t in range(TILES)]
        s_y = [sem(f"down{t}") for t in range(TILES)]
        s_ys = [sem(f"y_scaled{t}") for t in range(TILES)]
        s_acc = [sem(f"acc_added{t}") for t in range(TILES)]
        s_go = sem("gathers_begun")
        s_added = [sem(f"adds_begun{t}") for t in range(TILES)]
        o_free = sem("ov_expert_done")
        s_fin_in = [sem(f"acc_loaded{c}") for c in range(FIN_CHUNKS)]
        s_fin, s_out = sem("out_ready"), sem("out_stored")

        STK_A, STK_D, STK = (0, 0, 1, 2), (0, 1, 1, 2), (3, 3)

        def stack_bank(b, j):
            return bank[j] if b == 0 else bank[5]

        block = ctx.enter_context(nc.Block())

        def of_expert(w, e, pattern, **sizes):
            v = w.rearrange(pattern, **sizes)
            if isinstance(e, int):
                return v[e]
            return v[bass.ds(e, 1)].rearrange("a p c f -> (a p) c f")

        def load_weights(eng, e, r, done):
            eng.dma_start(wgu[:, r, :, 0:F], of_expert(w_gate, e, "e (c p) f -> e p c f", p=P)).then_inc(done, 16)
            eng.dma_start(wgu[:, r, :, F:2 * F], of_expert(w_up, e, "e (c p) f -> e p c f", p=P)).then_inc(done, 16)
            eng.dma_start(wd[:, r, :, :], of_expert(w_down, e, "e (c p) n -> e p c n", p=FH)).then_inc(done, 16)

        def experts(eng, body):
            body(0, 0)
            groups = (E - 1) // RING
            with eng.Fori(0, groups) as i:
                for j in range(RING):
                    body(i * RING + (j + 1), (j + 1) % RING)
            for e in range(1 + groups * RING, E):
                body(e, e % RING)

        @block.sync
        def _(sp):
            sp.dma_start(xs[:, 0, :], x[0]).then_inc(s_in[0], 16)
            sp.dma_start(qc[:, 0, 1, :], ctx_kv[0]).then_inc(s_in[0], 16)
            sp.dma_start(cst[:, :], consts[:, 0:C_SMALL]).then_inc(s_cst, 16)
            sp.dma_start(sel_in, consts[:, C_SMALL:C_END]).then_inc(s_sel, 16)
            for b in range(1, B):
                sp.dma_start(xs[:, b, :], x[b]).then_inc(s_in[b], 16)
                if b < QC:
                    sp.dma_start(qc[:, b, 1, :], ctx_kv[b]).then_inc(s_in[b], 16)
            sp.dma_start(wr_sb[:, :], wg_router).then_inc(s_wr, 16)
            sp.dma_start(wsg[:, :, :], ws_gate.rearrange("(c p) f -> p c f", p=P)).then_inc(s_wsh, 16)
            sp.dma_start(wsu[:, :, :], ws_up.rearrange("(c p) f -> p c f", p=P)).then_inc(s_wsh, 16)
            for c, (f0, n) in enumerate(FS_CHUNKS):
                sp.dma_start(wsd[0:n, c, :], ws_down[f0:f0 + n, :]).then_inc(s_wsh, 16)
            sp.wait_ge(s_row0, 2)
            sp.dma_start(list_dram.rearrange("(r p) w -> r (p w)", p=P), empty[:, :, :].rearrange("r p w -> r (p w)")).then_inc(s_init, 16)
            sp.wait_ge(s_zrow, 1)
            sp.dma_start(acc_dram[0][TOKENS:TOKENS + P, :], zero_row[:, :]).then_inc(s_acc0, 16)
            sp.dma_start(acc_dram[1].rearrange("(n p) r -> p n r", p=P),
                         zero_row[:, :].unsqueeze(1).to_broadcast([P, B + 1, T])).then_inc(s_acc0, 16)
            sp.dma_start(z_dram[TOKENS:TOKENS + P, :], zero_row[:, :]).then_inc(s_zst, 16)
            for b in range(QC, B):
                sp.wait_ge(s_vT, b - QC + 1)
                sp.wait_ge(s_qkn, b - QC + 1)
                sp.dma_start(qc[:, b % QC, 1, :], ctx_kv[b]).then_inc(s_in[b], 16)
            for b in range(B):
                sp.wait_ge(s_z, b + 1)
                sp.dma_start(z_dram[b * P:(b + 1) * P, :], z[:, b, :]).then_inc(s_zst, 16)
                if b == B - RING:
                    sp.wait_ge(s_vT, B)
                    sp.wait_ge(s_qkn, B)
                    for e in range(RING):
                        load_weights(sp, e, e, s_w_in[e])
            for b in range(B):
                sp.wait_ge(s_base, b + 1)
                sp.dma_start(acc_dram[0][b * P:(b + 1) * P, :], base[:, b % 2, :]).then_inc(s_seed[b % 2], 16)
                if b == 0:
                    sp.wait_ge(s_scat, 16 * TOPK * B)
                    sp.dma_start(slot_list[:, :, :].rearrange("r p w -> r (p w)"),
                                 list_dram.rearrange("(r p) w -> r (p w)", p=P)).then_inc(s_list, 16)
            with sp.Fori(0, E // RING - 1) as i:
                for r in range(RING):
                    sp.wait_ge(s_dh, i * RING + (r + 1))
                    sp.wait_ge(s_dl, i * RING + (r + 1))
                    load_weights(sp, i * RING + (r + RING), r, s_w_in[r])
            sp.wait_ge(s_flag, 1)
            n_max = sp.value_load(flag[0:1, 0:1], min_val=0, max_val=TOKENS)
            with sp.If(n_max > TILES * P):
                with sp.Fori(0, E) as e:
                    sp.wait_ge(o_free, e + 1)
                    load_weights(sp, e, 0, s_w_in[0])
                sp.wait_ge(o_free, E + 1)
            for t in range(TILES):
                sp.wait_ge(s_acc[t], 16 * E)
                for c in range(FIN_CHUNKS):
                    sp.dma_start(fin[:, c, t, :].rearrange("p (n r) -> p n r", r=T),
                                 acc_dram[t][c * per * P:(c + 1) * per * P, :].rearrange("(n p) r -> p n r", p=P)
                                 ).then_inc(s_fin_in[c], 16)
            for c in range(FIN_CHUNKS):
                sp.wait_ge(s_fin, c + 1)
                sp.dma_start(out[c * per:(c + 1) * per].rearrange("n p r -> p n r"),
                             fin[:, c, 0, :].rearrange("p (n r) -> p n r", r=T)).then_inc(s_out, 16)
            sp.wait_ge(s_out, 16 * FIN_CHUNKS)
            sp.wait_ge(s_acc0, 32)
            sp.wait_ge(s_init, 16)
            sp.wait_ge(s_zst, 16 * (B + 1))

        @block.tensor
        def _(pe):
            def sumsq(b):
                pe.wait_ge(s_sq, b + 1)
                if b >= 1:
                    pe.wait_ge(s_lnss, b)
                if b >= 6:
                    pe.wait_ge(s_prod, b - 5)
                pe.matmul(ss_ps, head_block, sq[:, b % 2, :], start=True, stop=True).then_inc(s_ss, 1)

            def turn_v(b):
                pe.wait_ge(s_in[b], 32)
                if b >= 4:
                    pe.wait_ge(s_zT, b - 3)
                    pe.wait_ge(s_ex, b - 3)
                elif b >= 1:
                    pe.wait_ge(s_vm, 2 * b)
                for c in range(KC):
                    last = pe.transpose(t_ps[:, c, :], qc[:, b % QC, 1, c * P:(c + 1) * P], ident)
                last.then_inc(s_vT, 1)

            def fill(b, j):
                if j == 0:
                    pe.wait_ge(s_hi, b + 1)
                    pe.wait_ge(s_lo, b + 1)
                if b >= 1:
                    pe.wait_ge(s_stk_a, STK_A[j] + STK[0] * b)
                    pe.wait_ge(s_stk_d, STK_D[j] + STK[1] * b)
                st_ps = stack_bank(b, j)
                is_q = j // 2
                for n in range(2):
                    pair = j % 2 * 2 + n
                    at = PAIRS * SELK_W + pair * SELQ_W if is_q else pair * SELK_W
                    shift = 2 * DH if is_q else DH
                    src = slice(0, T) if is_q else slice(T, 2 * T)
                    pe.matmul(st_ps[:, n * T:(n + 1) * T], sel[:, at + shift:at + shift + P], hi[:, b % 2, src],
                              start=True, stop=False)
                    last = pe.matmul(st_ps[:, n * T:(n + 1) * T], sel[:, at:at + P], lo[:, b % 2, src],
                                     start=False, stop=True)
                last.then_inc(s_fill, 1)

            def scores(b, i):
                n = b * PAIRS + i
                if i == 0:
                    pe.wait_ge(s_stk_a, STK[0] * (b + 1))
                    pe.wait_ge(s_stk_d, STK[1] * (b + 1))
                if n >= 2:
                    pe.wait_ge(s_p, n - 1)
                for c in range(KC):
                    last = pe.matmul(score_ps[:, i % 2, c, :], kst[:, b % 2, i, c * P:(c + 1) * P],
                                     qst[:, b % 2, i, :, :].rearrange("p a n -> p (a n)"), start=True, stop=True)
                last.then_inc(s_sc, 1)

            def pv(b, step):
                if step == 0:
                    pe.wait_ge(s_p, PAIRS * (b + 1))
                    pe.wait_ge(s_vm, 2 * (b + 1))
                    if b >= 1:
                        pe.wait_ge(s_att, b)
                        pe.wait_ge(s_lnden, b)
                den, parity = step >= 2, step % 2
                acc = den_ps if den else num_ps
                for c in range(KC):
                    for i in range(PAIRS):
                        q = 32 * i
                        w = ones_half[parity] if den else vm[:, b % 3, parity, c, q:q + 32]
                        last = pe.matmul(acc[q:q + 32, :], w, probs[:, b % 2, i, c, parity * T:(parity + 1) * T],
                                         start=(parity, c) == (0, 0), stop=(parity, c) == (1, KC - 1))
                if step == 3:
                    last.then_inc(s_pv, 1)

            def turn_z(b):
                pe.wait_ge(s_z, b + 1)
                pe.wait_ge(s_vm, 2 * min(b + 4, B))
                if b >= 1:
                    pe.wait_ge(s_ex, b)
                for c in range(KC):
                    last = pe.transpose(t_ps[:, c, :], z[:, b, c * P:(c + 1) * P], ident)
                last.then_inc(s_zps, 1)

            def logits(b):
                pe.wait_ge(s_zT, b + 1)
                for c in range(KC):
                    last = pe.matmul(logit_ps, zT[:, b, c, :], wrT[:, c, :], start=c == 0, stop=c == KC - 1)
                last.then_inc(s_lg, 1)

            def positions(b):
                pe.wait_ge(s_ch, b + 1)
                pe.wait_ge(s_bef, b + 1)
                pe.wait_ge(s_lnss, min(b + 6, B))
                if b >= 1:
                    pe.wait_ge(s_prod, b)
                pe.matmul(pos_ps, tri[:, :], chosen[:, b, :], start=True, stop=False)
                pe.matmul(pos_ps, ones_bf[:, :], before[:, b, :], start=False, stop=True).then_inc(s_pos, 1)

            def three_passes(ps, parts, first=True, last=True):
                for i, (x_part, w_part) in enumerate((parts[0:2], (parts[2], parts[1]), (parts[0], parts[3]))):
                    mm = pe.matmul(ps, x_part, w_part, start=first and i == 0, stop=last and i == 2)
                return mm

            def sh_turn(b):
                pe.wait_ge(s_h_s, b + 1)
                if b >= 2:
                    pe.wait_ge(s_hTl_s, b - 1)
                for c, (f0, n) in enumerate(FS_CHUNKS):
                    last = pe.transpose(bank[4 + b % 2][0:n, c * P:(c + 1) * P], hs[:, b % 2, f0:f0 + n], ident)
                last.then_inc(s_hps_s, 1)

            def sh_down(b):
                pe.wait_ge(s_hTh_s, 2 * (b + 1))
                pe.wait_ge(s_hTl_s, b + 1)
                if b >= 1:
                    pe.wait_ge(s_base, b)
                for c, (f0, n) in enumerate(FS_CHUNKS):
                    x_hi, x_lo = (hsT_r[0:n, b % 2, part, c * P:(c + 1) * P] for part in range(2))
                    last = three_passes(bank[6][:, 0:T], (x_hi, wsd_r[0:n, 0, c, :], x_lo, wsd_r[0:n, 1, c, :]), c == 0, c == 2)
                last.then_inc(s_y_s, 1)

            def sh_gate_up(b):
                pe.wait_ge(s_zh, b + 1)
                pe.wait_ge(s_zl, b + 1)
                if b >= 2:
                    pe.wait_ge(s_h_s, b - 1)
                for k in range(2):
                    for c in range(KC):
                        x_hi, x_lo = (z_r[:, b % 2, part, c * P:(c + 1) * P] for part in range(2))
                        last = three_passes(score_ps[:, b % 2, k, 0:FS],
                                            (x_hi, wsgu_r[:, 0, k, c, :], x_lo, wsgu_r[:, 1, k, c, :]), c == 0, c == KC - 1)
                last.then_inc(s_shps, 1)

            pe.wait_ge(s_cst, 16)
            sumsq(0)
            turn_v(0)
            pe.wait_ge(s_selc, 1)
            for j in range(4):
                fill(0, j)
            sumsq(1)
            pe.wait_ge(s_zero, 3)
            pe.wait_ge(s_setup, 2)
            for t in range(B + 2):
                for i in range(PAIRS):
                    if t < B:
                        scores(t, i)
                    if i == 0 and t + 2 < B:
                        sumsq(t + 2)
                    if t + 1 < B:
                        fill(t + 1, i)
                    if i == 1 and t + 1 < B:
                        turn_v(t + 1)
                    if i == 2 and t >= 2:
                        turn_z(t - 2)
                    if i == 3 and t >= 2:
                        logits(t - 2)
                    if t == 0 and i == PAIRS - 1:
                        pe.wait_ge(s_wr, 16)
                        for c in range(KC):
                            last = pe.transpose(bank[4][:, c * E:(c + 1) * E], wr_sb[:, c * P:(c + 1) * P], ident[0:E, 0:E])
                        last.then_inc(s_wrps, 1)
                    if t == 1 and i == 0:
                        pe.wait_ge(s_wrT, 1)
                    if 0 <= t - 1 < B:
                        pv(t - 1, i)
                    if i == (2 if t < B else 1) and t >= 3:
                        positions(t - 3)
                    if t == B and i == 3:
                        pe.wait_ge(s_wsh_lo, 4)
                        pe.wait_ge(s_p, PAIRS * B)
                        sh_gate_up(0)
                    if t == B + 1 and i == 0:
                        sh_gate_up(1)

            def turn_slots(e, r, par):
                pe.wait_ge(s_x_in[r], e // RING * 32 + 32 if isinstance(e, int) else (e - r) * (32 // RING) + 32)
                if not (isinstance(e, int) and e < 2):
                    pe.wait_ge(s_xl, e - 1)
                for t in range(TILES):
                    for c in range(KC):
                        k = t * KC + c
                        last = pe.transpose(bank[par][:, k * P:(k + 1) * P], slot[:, r, t, c * P:(c + 1) * P], ident)
                last.then_inc(s_xps, 1)

            pe.wait_ge(s_lnden, B)
            pe.wait_ge(s_att, B)
            sh_turn(0)
            sh_gate_up(2)
            sh_turn(1)
            positions(B - 1)
            pe.wait_ge(s_prod, B)
            pe.matmul(pos_ps, ones_bf[:, :], before[:, B - 1, :], start=True, stop=False)
            pe.matmul(pos_ps, ones_bf[:, :], chosen[:, B - 1, :], start=False, stop=True).then_inc(s_cnt, 1)
            pe.wait_ge(s_cmax, 1)
            sh_down(0)
            for b in range(3, B + 2):
                if b < B:
                    sh_gate_up(b)
                if b <= B:
                    sh_turn(b - 1)
                if b == B + 1:
                    pe.wait_ge(s_h_s, B)
                    turn_slots(0, 0, 0)
                sh_down(b - 2)
                if b == LIST_STEP:
                    pe.wait_ge(s_list, 16)
                    pe.wait_ge(s_ex, B)
                    for c in range(2):
                        last = pe.transpose(bank[7][:, c * P:c * P + E * TCAP], slot_list[:, :, c], ident[0:E * TCAP, 0:E * TCAP])
                    last.then_inc(s_lps, 1)

            def gate_up(e, r, par, t):
                if t == 0:
                    pe.wait_ge(s_gh, e + 1)
                    pe.wait_ge(s_gl, e + 1)
                    pe.wait_ge(s_xl, e + 1)
                if not (isinstance(e, int) and e == 0):
                    pe.wait_ge(s_h[t], e)
                for c in range(KC):
                    k = (t * KC + c) * P
                    last = three_passes(bank[2 + t][:, 0:2 * F],
                                        (slotT_hi[:, par, k:k + P], wgu_r[:, par, 0, c, :],
                                         slotT_lo[:, par, k:k + P], wgu_r[:, par, 1, c, :]), c == 0, c == KC - 1)
                last.then_inc(s_gu[t], 1)

            def turn_hidden(e, t):
                pe.wait_ge(s_h[t], e + 1)
                if not (isinstance(e, int) and e == 0):
                    pe.wait_ge(s_hTl[t], e)
                for c in range(2):
                    last = pe.transpose(bank[4 + t][0:FH, c * P:(c + 1) * P], h[:, t, c * FH:(c + 1) * FH], ident)
                last.then_inc(s_hps[t], 1)

            def down(e, r, t):
                if t == 0:
                    pe.wait_ge(s_dh, e + 1)
                    pe.wait_ge(s_dl, e + 1)
                pe.wait_ge(s_hTl[t], e + 1)
                if not (isinstance(e, int) and e == 0):
                    pe.wait_ge(s_ys[t], e)
                for c in range(2):
                    last = three_passes(bank[6 + t][:, 0:T],
                                        (hT_r[:, t, 0, c * P:(c + 1) * P], wd_r[:, r % 2, 0, c, :],
                                         hT_r[:, t, 1, c * P:(c + 1) * P], wd_r[:, r % 2, 1, c, :]), c == 0, c == 1)
                last.then_inc(s_y[t], 1)

            pe.wait_ge(s_h_s, B)
            pe.wait_ge(s_hTl_s, B)
            pe.wait_ge(s_base, B)
            pe.wait_ge(s_cmax, 1)

            def expert(e, r):
                first, final = isinstance(e, int) and e == 0, isinstance(e, int) and e == E - 1
                if not final:
                    turn_slots(e + 1, (r + 1) % RING, (r + 1) % 2)
                gate_up(e, r, r % 2, 0)
                if not first:
                    turn_hidden(e - 1, 1)
                    down(e - 1, (r - 1) % RING, 0)
                gate_up(e, r, r % 2, 1)
                turn_hidden(e, 0)
                if not first:
                    down(e - 1, (r - 1) % RING, 1)

            experts(pe, expert)
            turn_hidden(E - 1, 1)
            down(E - 1, (E - 1) % RING, 0)
            down(E - 1, (E - 1) % RING, 1)

            pe.wait_ge(s_flag, 1)
            n_max = pe.value_load(flag[0:1, 0:1], min_val=0, max_val=TOKENS)
            with pe.If(n_max > TILES * P):
                for t in range(TILES):
                    pe.wait_ge(s_ys[t], E)
                with pe.Fori(0, E) as e:
                    pe.wait_ge(s_x_in[0], e * 16 + (32 * (E // RING) + 16))
                    for c in range(KC):
                        last = pe.transpose(bank[0][:, c * P:(c + 1) * P], slot[:, 0, 0, c * P:(c + 1) * P], ident)
                    last.then_inc(s_xps, 1)
                    pe.wait_ge(s_xl, e + (E + 1))
                    pe.wait_ge(s_w_in[0], e * 48 + 48 * (E // RING + 1))
                    for c in range(KC):
                        last = pe.matmul(bank[2][:, 0:2 * F], slotT[:, c * P:(c + 1) * P], wgu[:, 0, c, :],
                                         start=c == 0, stop=c == KC - 1)
                    last.then_inc(s_gu[0], 1)
                    pe.wait_ge(s_h[0], e + (E + 1))
                    for c in range(2):
                        last = pe.transpose(bank[4][0:FH, c * P:(c + 1) * P], h[:, 0, c * FH:(c + 1) * FH], ident)
                    last.then_inc(s_hps[0], 1)
                    pe.wait_ge(s_hTl[0], e + (E + 1))
                    for c in range(2):
                        last = pe.matmul(bank[6][:, 0:T], hT[:, c * P:(c + 1) * P], wd[:, 0, c, :], start=c == 0, stop=c == 1)
                    last.then_inc(s_y[0], 1)

        @block.scalar
        def _(act):
            def inv_norms(b):
                act.wait_ge(s_ss, b + 1)
                if b >= 2:
                    act.wait_ge(s_qkn, b - 1)
                act.activation(rn[:, b % 2, :], ss_ps, ACT.Ln, bias=ln_floor, scale=SHIFT).then_inc(s_lnss, 1)
                act.wait_ge(s_lnss, b + 1)
                act.activation(rn[:, b % 2, :], rn[:, b % 2, :], ACT.Exp, scale=-0.5).then_inc(s_rn, 1)

            def high_part(b):
                act.wait_ge(s_qkn, b + 1)
                if b >= 2:
                    act.wait_ge(s_fill, 4 * (b - 1))
                act.copy(hi[:, b % 2, :], qkn[:, b % 2, :]).then_inc(s_hi, 1)

            def copy_stack(b, j):
                act.wait_ge(s_fill, 4 * b + j + 1)
                if b >= 2 and j == 1:
                    act.wait_ge(s_sc, PAIRS * (b - 1))
                pairs = slice(j % 2 * 2, j % 2 * 2 + 2)
                src = stack_bank(b, j).rearrange("p (i n) -> p i n", i=2)
                if j == 1:
                    act.copy(kst[:, b % 2, pairs, :], src).then_inc(s_stk_a, 1)
                else:
                    act.copy(qst[0:64, b % 2, pairs, 0, :], src[0:64]).then_inc(s_stk_a, 1)

            def copy_v(b):
                act.wait_ge(s_vT, b + 1)
                if b >= 3:
                    act.wait_ge(s_pv, b - 2)
                for parity in range(2):
                    heads = "p c (i a d) -> p c i a d"
                    src = t_ps.rearrange(heads, i=PAIRS, a=2)[:, :, :, parity, :]
                    dst = vm[:, b % 3, parity, :, :].rearrange(heads, i=PAIRS, a=2)[:, :, :, parity, :]
                    act.copy(dst, src).then_inc(s_vm, 1)

            def exp_scores(b, i):
                act.wait_ge(s_sc, b * PAIRS + i + 1)
                if b >= 2 and i == 0:
                    act.wait_ge(s_pv, b - 1)
                act.activation(probs[:, b % 2, i, :, :], score_ps[:, i % 2, :, :], ACT.Exp,
                               scale=ALPHA * UNSHIFT * UNSHIFT).then_inc(s_p, 1)

            def inv_den(b):
                act.wait_ge(s_pv, b + 1)
                act.activation(lnden[:, b % 2, :], den_ps, ACT.Ln).then_inc(s_lnden, 1)
                act.wait_ge(s_lnden, b + 1)
                if b >= 2:
                    act.wait_ge(s_att, b - 1)
                act.activation(rden[:, b % 2, :], lnden[:, b % 2, :], ACT.Exp, scale=-1.0).then_inc(s_rden, 1)

            def z_high(b):
                act.wait_ge(s_zT, b + 1)
                if b >= 2:
                    act.wait_ge(s_shps, b - 1)
                    act.wait_ge(s_zl, b - 1)
                act.copy(z_r[:, b % 2, 0, :], zT[:, b, :, :].rearrange("p c n -> p (c n)")).then_inc(s_zh, 1)

            def exp_logits(b):
                act.wait_ge(s_lg, b + 1)
                act.wait_ge(s_negm, b + 1)
                act.activation(ex[:, b, :], logit_ps, ACT.Exp, bias=negm[:, b:b + 1],
                               accum_out=esum[:, b:b + 1]).then_inc(s_ex, 1)

            act.dma_start(gates[:, 0:1], g_xattn.partition_broadcast(P)).then_inc(s_gate, 16)
            act.dma_start(gates[:, 1:2], g_ffn.partition_broadcast(P)).then_inc(s_gate, 16)
            def sh_silu(b):
                act.wait_ge(s_shps, b + 1)
                if b >= 2:
                    act.wait_ge(s_h_s, b - 1)
                act.activation(sgs[:, b % 2, :], score_ps[:, b % 2, 0, 0:FS], ACT.Silu).then_inc(s_sg_s, 1)

            def sh_hidden_high(b):
                act.wait_ge(s_hps_s, b + 1)
                if b >= 2:
                    act.wait_ge(s_y_s, b - 1)
                k = b % 2
                act.copy(hsT_r[:, k, 0, 0:2 * P], bank[4 + k][:, 0:2 * P]).then_inc(s_hTh_s, 1)
                act.copy(hsT_r[0:96, k, 0, 2 * P:3 * P], bank[4 + k][0:96, 2 * P:3 * P]).then_inc(s_hTh_s, 1)

            act.wait_ge(s_gate, 32)
            act.activation(tg[:, :], gates[:, :], ACT.Tanh).then_inc(s_tg, 1)
            act.preload_act_table_set("natural_log_exp_and_others")
            act.wait_ge(s_cst, 16)
            inv_norms(0)
            high_part(0)
            act.wait_ge(s_zero, 1)
            copy_v(0)
            for j in range(1, 4):
                copy_stack(0, j)
            inv_norms(1)
            for t in range(B + 2):
                if t >= 2:
                    inv_den(t - 2)
                if t == B + 1:
                    sh_silu(0)
                    sh_silu(1)
                    z_high(2)
                    act.preload_act_table_set("natural_log_exp_and_others")
                for i in range(PAIRS):
                    if t < B:
                        exp_scores(t, i)
                    if t == 0 and i == 0:
                        high_part(1)
                    if t == 0 and i == PAIRS - 1:
                        act.wait_ge(s_wrps, 1)
                        act.copy(wrT[:, :, :].rearrange("p c e -> p (c e)"), bank[4][:, 0:KC * E]).then_inc(s_wrT, 1)
                    if i >= 1 and t + 1 < B:
                        copy_stack(t + 1, i)
                    if i == 0 and t + 2 < B:
                        inv_norms(t + 2)
                    if i == 1 and t + 1 < B:
                        copy_v(t + 1)
                    if i == 2 and t + 2 < B:
                        high_part(t + 2)
                if t >= 2:
                    exp_logits(t - 2)
                if t == B - 1:
                    z_high(0)
                    z_high(1)

            def gate_up_high(e, r, par):
                act.wait_ge(s_w_in[r], e // RING * 48 + 48 if isinstance(e, int) else (e - r) * (48 // RING) + 48)
                if not (isinstance(e, int) and e < 2):
                    act.wait_ge(s_gu[TILES - 1], e - 1)
                act.copy(wgu_r[:, par, 0, :, :], wgu[:, r, :, :]).then_inc(s_gh, 1)

            sh_hidden_high(0)
            z_high(3)
            for b in range(2, B + 1):
                if b < B:
                    sh_silu(b)
                if b + 2 < B:
                    z_high(b + 2)
                sh_hidden_high(b - 1)
                if b == B - 1:
                    gate_up_high(0, 0, 0)

            def silu(e, t):
                act.wait_ge(s_gu[t], e + 1)
                if not (isinstance(e, int) and e == 0):
                    act.wait_ge(s_h[t], e)
                act.activation(sg[:, t, :], bank[2 + t][:, 0:F], ACT.Silu).then_inc(s_sg[t], 1)

            def hidden_high(e, t):
                act.wait_ge(s_hps[t], e + 1)
                if not (isinstance(e, int) and e == 0):
                    act.wait_ge(s_y[t], e)
                act.copy(hT_r[:, t, 0, :], bank[4 + t][0:FH, 0:2 * P]).then_inc(s_hTh[t], 1)

            def slots_high(e, par):
                act.wait_ge(s_xps, e + 1)
                if not (isinstance(e, int) and e < 2):
                    act.wait_ge(s_gu[TILES - 1], e - 1)
                act.copy(slotT_hi[:, par, :], bank[par]).then_inc(s_xh, 1)

            def down_high(e, r):
                if not (isinstance(e, int) and e == 0):
                    act.wait_ge(s_y[0], e)
                act.copy(wd_r[:, r % 2, 0, :, :], wd[:, r, :, :]).then_inc(s_dh, 1)

            slots_high(0, 0)

            def expert(e, r):
                first, final = isinstance(e, int) and e == 0, isinstance(e, int) and e == E - 1
                if not final:
                    slots_high(e + 1, (r + 1) % 2)
                silu(e, 0)
                if not first:
                    hidden_high(e - 1, 1)
                if not final:
                    gate_up_high(e + 1, (r + 1) % RING, (r + 1) % 2)
                silu(e, 1)
                down_high(e, r)
                hidden_high(e, 0)

            experts(act, expert)
            hidden_high(E - 1, 1)

            act.wait_ge(s_flag, 1)
            n_max = act.value_load(flag[0:1, 0:1], min_val=0, max_val=TOKENS)
            with act.If(n_max > TILES * P):
                with act.Fori(0, E) as e:
                    act.wait_ge(s_gu[0], e + (E + 1))
                    act.activation(sg[:, 0, :], bank[2][:, 0:F], ACT.Silu).then_inc(s_sg[0], 1)
                    act.wait_ge(s_hps[0], e + (E + 1))
                    act.copy(hT, bank[4][0:FH, 0:2 * P]).then_inc(s_hTl[0], 1)

        @block.vector
        def _(dve):
            def stats1(b):
                if b < B:
                    dve.wait_ge(s_in[b], 32)
                    dve.bn_stats(st1[:, b, :], xs[:, b, :]).then_inc(s_st1, 1)

            def mean_var1(b):
                if b < B:
                    dve.wait_ge(s_st1, b + 1)
                    dve.bn_aggr(mv1[:, b, :], st1[:, b, :]).then_inc(s_mv1, 1)

            def ln1_stats(b):
                stats1(b)
                mean_var1(b)

            def ln1(b):
                if b >= B:
                    return
                dve.wait_ge(s_rstd1, b + 1)
                if b >= QC:
                    dve.wait_ge(s_qkn, b - QC + 1)
                dve.tensor_scalar(qc[:, b % QC, 0, :], xs[:, b, :], mv1[:, b, 0:1], rstd1[:, b:b + 1],
                                  ALU.subtract, ALU.mult).then_inc(s_q, 1)

            def squares(b):
                if b >= B:
                    return
                dve.wait_ge(s_q, b + 1)
                if b >= 2:
                    dve.wait_ge(s_ss, b - 1)
                qcb = qc[:, b % QC, :, :].rearrange("p a n -> p (a n)")
                dve.tensor_tensor(sq[:, b % 2, :], qcb, qcb, ALU.mult).then_inc(s_sq, 1)

            def q_and_squares(b):
                ln1(b)
                squares(b)

            def normalise(b):
                if b >= B:
                    return
                dve.wait_ge(s_rn, b + 1)
                if b >= 2:
                    dve.wait_ge(s_hi, b - 1)
                    dve.wait_ge(s_lo, b - 1)
                dve.scalar_tensor_tensor(out=qkn[:, b % 2, :], in0=rn[:, b % 2, :], scalar=1 / NORM_EPS / UNSHIFT,
                                         in1=qc[:, b % QC, :, :].rearrange("p a n -> p (a n)"),
                                         op0=ALU.min, op1=ALU.mult).then_inc(s_qkn, 1)

            def copy_stack(b, j):
                if b >= B:
                    return
                dve.wait_ge(s_fill, 4 * b + j + 1)
                if b >= 2 and j == 0:
                    dve.wait_ge(s_sc, PAIRS * (b - 1))
                pairs = slice(j % 2 * 2, j % 2 * 2 + 2)
                src = stack_bank(b, j).rearrange("p (i n) -> p i n", i=2)
                if j == 0:
                    dve.tensor_copy(kst[:, b % 2, pairs, :], src).then_inc(s_stk_d, 1)
                else:
                    dve.tensor_copy(qst[64:P, b % 2, pairs, 1, :], src[64:P]).then_inc(s_stk_d, 1)

            def live(b):
                return 0 <= b < B

            def att_over_den(b):
                if live(b):
                    dve.wait_ge(s_rden, b + 1)
                    if b >= 2:
                        dve.wait_ge(s_x2, b - 1)
                    dve.tensor_tensor(att[:, b % 2, :], num_ps, rden[:, b % 2, :], ALU.mult).then_inc(s_att, 1)

            def add_residual(b):
                if live(b):
                    dve.wait_ge(s_att, b + 1)
                    dve.scalar_tensor_tensor(out=x2[:, b, :], in0=att[:, b % 2, :], scalar=tg[:, 0:1], in1=xs[:, b, :],
                                             op0=ALU.mult, op1=ALU.add).then_inc(s_x2, 1)

            def copy_zT(b):
                if live(b):
                    dve.wait_ge(s_zps, b + 1)
                    dve.tensor_copy(zT[:, b, :, :], t_ps).then_inc(s_zT, 1)

            def stats2(b):
                if live(b):
                    dve.wait_ge(s_x2, b + 1)
                    dve.bn_stats(st2[:, b, :], x2[:, b, :]).then_inc(s_st2, 1)

            def mean_var2(b):
                if live(b):
                    dve.wait_ge(s_st2, b + 1)
                    dve.bn_aggr(mv2[:, b, :], st2[:, b, :]).then_inc(s_mv2, 1)

            def ln2(b):
                if live(b):
                    dve.wait_ge(s_rstd2, b + 1)
                    dve.tensor_scalar(z[:, b, :], x2[:, b, :], mv2[:, b, 0:1], rstd2[:, b:b + 1],
                                      ALU.subtract, ALU.mult).then_inc(s_z, 1)

            def top_logit(b):
                if live(b):
                    dve.wait_ge(s_lg, b + 1)
                    dve.max(m8[:, b, :], logit_ps).then_inc(s_m8, 1)

            def neg_top_logit(b):
                if live(b):
                    dve.wait_ge(s_m8, b + 1)
                    dve.tensor_scalar(negm[:, b:b + 1], m8[:, b, 0:1], -1.0, None, ALU.mult).then_inc(s_negm, 1)

            def inv_sum(b):
                if live(b):
                    dve.wait_ge(s_ex, b + 1)
                    dve.reciprocal(rsum[:, b:b + 1], esum[:, b:b + 1]).then_inc(s_rsum, 1)

            def router_score(b):
                if live(b):
                    dve.wait_ge(s_rsum, b + 1)
                    dve.tensor_scalar(score[:, b, :], ex[:, b, :], rsum[:, b:b + 1], None, ALU.mult).then_inc(s_score, 1)

            def top_scores(b):
                if live(b):
                    dve.wait_ge(s_score, b + 1)
                    dve.max(v8[:, b, :], score[:, b, :]).then_inc(s_v8, 1)

            def top_experts(b):
                if live(b):
                    dve.wait_ge(s_v8, b + 1)
                    dve.max_index(idx8[:, b, :], v8[:, b, :], score[:, b, :]).then_inc(s_idx, 1)
                    dve.tensor_reduce(wsum[:, b:b + 1], v8[:, b, 0:TOPK], AX.X, ALU.add).then_inc(s_wsum, 1)

            def experts_as_floats(b):
                if live(b):
                    dve.wait_ge(s_idx, b + 1)
                    dve.tensor_copy(idxf[:, b, :], idx8[:, b, 0:TOPK]).then_inc(s_idxf, 1)
                    dve.wait_ge(s_wsum, b + 1)
                    dve.tensor_scalar(wsum[:, b:b + 1], wsum[:, b:b + 1], 1e-20, None, ALU.add).then_inc(s_weps, 1)

            def one_hots(b):
                if live(b):
                    dve.wait_ge(s_idxf, b + 1)
                    if b >= 2:
                        dve.wait_ge(s_prod, b - 1)
                    dve.tensor_tensor(onehot[:, b % 2, :, :], iota_e.unsqueeze(1).to_broadcast([P, TOPK, E]),
                                      idxf[:, b, :].unsqueeze(2).to_broadcast([P, TOPK, E]), ALU.is_equal).then_inc(s_oh, 1)
                    dve.wait_ge(s_weps, b + 1)
                    dve.reciprocal(wrec[:, b:b + 1], wsum[:, b:b + 1]).then_inc(s_wrec, 1)

            def chosen_experts(b):
                if live(b):
                    dve.wait_ge(s_oh, b + 1)
                    with nc.allow_low_precision(reason="sums of ones and zeros, at most 1"):
                        dve.tensor_reduce(chosen[:, b, :], onehot[:, b % 2, :, :].rearrange("p k e -> p e k"),
                                          AX.X, ALU.add).then_inc(s_ch, 1)
                    if b + 1 < B:
                        dve.wait_ge(s_ch, b + 1)
                        dve.wait_ge(s_bef, b + 1)
                        dve.tensor_tensor(before[:, b + 1, :], before[:, b, :], chosen[:, b, :], ALU.add).then_inc(s_bef, 1)
                    dve.wait_ge(s_wrec, b + 1)
                    dve.tensor_scalar(wgate[:, b:b + 1], wrec[:, b:b + 1], tg[:, 1:2], None, ALU.mult).then_inc(s_wg, 1)

            def weights(b):
                if live(b):
                    dve.wait_ge(s_wg, b + 1)
                    if b == 0:
                        dve.wait_ge(s_pconst, 1)
                    dve.tensor_scalar(pairs[:, b, :, 1], v8[:, b, 0:TOPK], wgate[:, b:b + 1], None, ALU.mult).then_inc(s_w, 1)

            def chosen_positions(b):
                if live(b):
                    dve.wait_ge(s_pos, b + 1)
                    if b >= 2:
                        dve.wait_ge(s_posk, b - 1)
                    dve.tensor_tensor(prod[:, b % 2, :, :], onehot[:, b % 2, :, :],
                                      pos_ps.unsqueeze(1).to_broadcast([P, TOPK, E]), ALU.mult).then_inc(s_prod, 1)

            def position_sums(b):
                if live(b):
                    dve.wait_ge(s_prod, b + 1)
                    dve.tensor_reduce(posk[:, b, :], prod[:, b % 2, :, :], AX.X, ALU.add).then_inc(s_posk, 1)

            def over_capacity(b):
                if live(b):
                    dve.wait_ge(s_posk, b + 1)
                    dve.tensor_scalar(over[:, b, :], posk[:, b, :], float(CAP), float(E * CAP), ALU.is_ge, ALU.mult).then_inc(s_over, 1)
                    dve.scalar_tensor_tensor(out=dest_f[:, b, :], in0=idxf[:, b, :], scalar=float(CAP), in1=posk[:, b, :],
                                             op0=ALU.mult, op1=ALU.add).then_inc(s_d1, 1)

            def destinations(b):
                if live(b):
                    dve.wait_ge(s_over, b + 1)
                    dve.wait_ge(s_d1, b + 1)
                    dve.tensor_tensor(dest[:, b, :], dest_f[:, b, :], over[:, b, :], ALU.add).then_inc(s_dest, 1)

            def z_low(b):
                dve.wait_ge(s_zh, b + 1)
                if b >= 2:
                    dve.wait_ge(s_shps, b - 1)
                dve.tensor_tensor(z_r[:, b % 2, 1, :], zT[:, b, :, :].rearrange("p c n -> p (c n)"),
                                  z_r[:, b % 2, 0, :].bitcast(F32), ALU.subtract).then_inc(s_zl, 1)

            def sh_hidden(b):
                dve.wait_ge(s_sg_s, b + 1)
                if b >= 2:
                    dve.wait_ge(s_hps_s, b - 1)
                dve.tensor_tensor(hs[:, b % 2, :], score_ps[:, b % 2, 1, 0:FS], sgs[:, b % 2, :], ALU.mult).then_inc(s_h_s, 1)

            def sh_hidden_low(b):
                k = b % 2
                dve.wait_ge(s_hTh_s, 2 * (b + 1))
                if b >= 2:
                    dve.wait_ge(s_y_s, b - 1)
                dve.tensor_tensor(hsT_r[:, k, 1, 0:2 * P], bank[4 + k][:, 0:2 * P], hsT_r[:, k, 0, 0:2 * P].bitcast(F32), ALU.subtract)
                dve.tensor_tensor(hsT_r[0:96, k, 1, 2 * P:3 * P], bank[4 + k][0:96, 2 * P:3 * P],
                                  hsT_r[0:96, k, 0, 2 * P:3 * P].bitcast(F32), ALU.subtract).then_inc(s_hTl_s, 1)

            def sh_base(b):
                dve.wait_ge(s_y_s, b + 1)
                if b >= 2:
                    dve.wait_ge(s_seed[b % 2], 16 * (b // 2))
                dve.scalar_tensor_tensor(out=base[:, b % 2, :], in0=bank[6][:, 0:T], scalar=tg[:, 1:2],
                                         in1=x2[:, b, :], op0=ALU.mult, op1=ALU.add).then_inc(s_base, 1)

            def tokens(e):
                at = e * TCAP
                return slot_tok[:, at:at + TILES] if isinstance(e, int) else slot_tok[:, bass.ds(at, TILES)]

            def gather_tokens(e, r):
                dve.tensor_copy(tok_g[:, r, :], tokens(e)).then_inc(s_tokg, 1)

            ln1_stats(0)
            q_and_squares(0)
            dve.memset(ones_bf[:, :], 1.0).then_inc(s_setup, 1)
            dve.memset(zero_row[:, :], 0.0).then_inc(s_zrow, 1)
            dve.wait_ge(s_cst, 16)
            dve.tensor_copy(tri[:, :], cst[:, C_TRI:C_TRI + P]).then_inc(s_setup, 1)
            ln1_stats(1)
            dve.wait_ge(s_sel, 16)
            dve.tensor_copy(sel[:, :], sel_in).then_inc(s_selc, 1)
            normalise(0)
            q_and_squares(1)
            dve.wait_ge(s_hi, 1)
            dve.tensor_tensor(lo[:, 0, :], qkn[:, 0, :], hi[:, 0, :].bitcast(F32), ALU.subtract).then_inc(s_lo, 1)
            copy_stack(0, 0)
            copy_stack(0, 2)
            copy_stack(0, 3)
            ln1_stats(2)
            normalise(1)
            q_and_squares(2)
            dve.memset(empty[:, :, :], 0.0).then_inc(s_row0, 1)
            dve.wait_ge(s_row0, 1)
            dve.tensor_scalar(empty[:, :, 0], iota[0:E * TCAP, :], float(TOKENS), None, ALU.add).then_inc(s_row0, 1)
            dve.wait_ge(s_tg, 1)
            for t in range(B + 3):
                att_over_den(t - 2)
                inv_sum(t - 3)
                add_residual(t - 2)
                router_score(t - 3)
                stats2(t - 2)
                top_scores(t - 3)
                mean_var2(t - 2)
                copy_stack(t + 1, 0)
                top_experts(t - 3)
                stats1(t + 3)
                experts_as_floats(t - 3)
                mean_var1(t + 3)
                one_hots(t - 3)
                normalise(t + 2)
                chosen_experts(t - 3)
                ln2(t - 2)
                if t == B + 1:
                    sh_hidden(0)
                weights(t - 3)
                if t == B + 1:
                    sh_hidden(1)
                    z_low(2)
                copy_stack(t + 1, 2)
                ln1(t + 3)
                if t < B:
                    copy_zT(t - 2)
                chosen_positions(t - 3)
                if t >= B:
                    copy_zT(t - 2)
                squares(t + 3)
                position_sums(t - 3)
                copy_stack(t + 1, 3)
                top_logit(t - 2)
                over_capacity(t - 3)
                neg_top_logit(t - 2)
                destinations(t - 3)
                if t == B - 1:
                    z_low(0)
                    z_low(1)
            dve.wait_ge(s_cnt, 1)
            dve.tensor_reduce(cmax[:, :], pos_ps, AX.X, ALU.max).then_inc(s_cmax, 1)
            dve.wait_ge(s_cmax, 1)
            dve.tensor_copy(flag[:, :], cmax[:, :]).then_inc(s_flag, 1)

            def gate_up_low(e, r, par):
                dve.wait_ge(s_gh, e + 1)
                if not (isinstance(e, int) and e < 2):
                    dve.wait_ge(s_gu[TILES - 1], e - 1)
                dve.tensor_tensor(wgu_r[:, par, 1, :, :], wgu[:, r, :, :], wgu_r[:, par, 0, :, :].bitcast(F32), ALU.subtract).then_inc(s_gl, 1)

            def slots_low(e, par):
                dve.wait_ge(s_xh, e + 1)
                if not (isinstance(e, int) and e < 2):
                    dve.wait_ge(s_gu[TILES - 1], e - 1)
                dve.tensor_tensor(slotT_lo[:, par, :], bank[par], slotT_hi[:, par, :].bitcast(F32), ALU.subtract).then_inc(s_xl, 1)

            sh_hidden_low(0)
            z_low(3)
            for b in range(2, B + 2):
                if b < B:
                    sh_hidden(b)
                if b + 2 < B:
                    z_low(b + 2)
                if b <= B:
                    sh_hidden_low(b - 1)
                if b == LIST_STEP + 1:
                    dve.wait_ge(s_lps, 1)
                    dve.tensor_copy(slot_tok[:, :], bank[7][:, 0:E * TCAP]).then_inc(s_tok, 1)
                    dve.tensor_copy(slot_w[:, :], bank[7][:, P:P + E * TCAP]).then_inc(s_tok, 1)
                    dve.wait_ge(s_tok, 2)
                    for e in range(RING - 1):
                        gather_tokens(e, e)
                if b == B + 1:
                    slots_low(0, 0)
                sh_base(b - 2)
                if b == B - 1:
                    gate_up_low(0, 0, 0)

            def down_low(e, r):
                dve.wait_ge(s_dh, e + 1)
                if not (isinstance(e, int) and e == 0):
                    dve.wait_ge(s_y[0], e)
                dve.tensor_tensor(wd_r[:, r % 2, 1, :, :], wd[:, r, :, :], wd_r[:, r % 2, 0, :, :].bitcast(F32), ALU.subtract).then_inc(s_dl, 1)

            def hidden_low(e, t):
                dve.wait_ge(s_hTh[t], e + 1)
                if not (isinstance(e, int) and e == 0):
                    dve.wait_ge(s_y[t], e)
                dve.tensor_tensor(hT_r[:, t, 1, :], bank[4 + t][0:FH, 0:2 * P], hT_r[:, t, 0, :].bitcast(F32), ALU.subtract).then_inc(s_hTl[t], 1)

            def hidden(e, t):
                dve.wait_ge(s_sg[t], e + 1)
                if not (isinstance(e, int) and e == 0):
                    dve.wait_ge(s_hps[t], e)
                dve.tensor_tensor(h[:, t, :], bank[2 + t][:, F:2 * F], sg[:, t, :], ALU.mult).then_inc(s_h[t], 1)

            def scale_y(e, r, t):
                dve.wait_ge(s_y[t], e + 1)
                dve.wait_ge(s_added[t], e + 1)
                at = e * TCAP + t
                w = slot_w[:, at:at + 1] if isinstance(e, int) else slot_w[:, bass.ds(at, 1)]
                dve.tensor_scalar(ysc[:, r, t, :], bank[6 + t][:, 0:T], w, None, ALU.mult).then_inc(s_ys[t], 1)

            def scale_first_y(e, r):
                for t in range(1, TILES):
                    dve.wait_ge(s_added[t], e + 1)
                scale_y(e, r, 0)
                dve.tensor_copy(tok_a[:, r, :], tokens(e)).then_inc(s_toka, 1)


            def expert(e, r):
                first, final = isinstance(e, int) and e == 0, isinstance(e, int) and e == E - 1
                if not final:
                    slots_low(e + 1, (r + 1) % 2)
                if not (isinstance(e, int) and e >= E - RING + 1):
                    gather_tokens(e + RING - 1, (r - 1) % RING)
                hidden(e, 0)
                if not first:
                    hidden_low(e - 1, 1)
                if not final:
                    gate_up_low(e + 1, (r + 1) % RING, (r + 1) % 2)
                if not first:
                    scale_first_y(e - 1, (r - 1) % RING)
                hidden(e, 1)
                down_low(e, r)
                hidden_low(e, 0)
                if not first:
                    scale_y(e - 1, (r - 1) % RING, 1)

            experts(dve, expert)
            hidden_low(E - 1, 1)
            scale_first_y(E - 1, (E - 1) % RING)
            scale_y(E - 1, (E - 1) % RING, 1)

            dve.wait_ge(s_flag, 1)
            n_max = dve.value_load(flag[0:1, 0:1], min_val=0, max_val=TOKENS)
            with dve.If(n_max > TILES * P):
                with dve.Fori(0, E) as e:
                    dve.wait_ge(s_xps, e + (E + 1))
                    dve.tensor_copy(slotT[:, 0:T], bank[0][:, 0:T]).then_inc(s_xl, 1)
                    dve.wait_ge(s_sg[0], e + (E + 1))
                    dve.tensor_tensor(h[:, 0, :], bank[2][:, F:2 * F], sg[:, 0, :], ALU.mult).then_inc(s_h[0], 1)
                    dve.wait_ge(s_y[0], e + (E + 1))
                    dve.tensor_scalar(ysc[:, 0, 0, :], bank[6][:, 0:T], slot_w[:, bass.ds(e * TCAP + TILES, 1)], None,
                                      ALU.mult).then_inc(s_ys[0], 1)
            for c in range(FIN_CHUNKS):
                dve.wait_ge(s_fin_in[c], 32)
                dve.tensor_tensor(fin[:, c, 0, :], fin[:, c, 0, :], fin[:, c, 1, :], ALU.add).then_inc(s_fin, 1)

        @block.gpsimd
        def _(pool):
            pool.memset(minus_half, -0.5).then_inc(s_fills0, 1)
            pool.memset(before[:, 0, :], 0.0).then_inc(s_bef, 1)
            pool.wait_ge(s_fills0, 1)
            pool.memset(pairs[:, :, :, :], 0.0).then_inc(s_fills0, 1)
            pool.memset(vm[:, :, :, :, :], 0.0).then_inc(s_zero, 1)
            def rstd(b, s_mv, mv, s_ve, ve, s_rs, rs):
                pool.wait_ge(s_mv, b + 1)
                pool.tensor_scalar(ve[:, b:b + 1], mv[:, b, 1:2], LN_EPS, None, ALU.add).then_inc(s_ve, 1)
                pool.wait_ge(s_ve, b + 1)
                pool.tensor_tensor(rs[:, b:b + 1], ve[:, b:b + 1], minus_half, ALU.pow).then_inc(s_rs, 1)

            def low_part(b):
                pool.wait_ge(s_hi, b + 1)
                if b >= 2:
                    pool.wait_ge(s_fill, 4 * (b - 1))
                pool.tensor_tensor(lo[:, b % 2, :], qkn[:, b % 2, :], hi[:, b % 2, :].bitcast(F32), ALU.subtract).then_inc(s_lo, 1)

            def split_shared(i):
                pool.wait_ge(s_wsh, 80)
                whole = ((wsg[:, :, :], wsgu_r[:, 0, 0, :, :], wsgu_r[:, 1, 0, :, :]),
                         (wsu[:, :, :], wsgu_r[:, 0, 1, :, :], wsgu_r[:, 1, 1, :, :]),
                         (wsd[:, 0:2, :], wsd_r[:, 0, 0:2, :], wsd_r[:, 1, 0:2, :]),
                         (wsd[0:96, 2, :], wsd_r[0:96, 0, 2, :], wsd_r[0:96, 1, 2, :]))[i]
                w, w_hi, w_lo = whole
                pool.tensor_copy(w_hi, w).then_inc(s_wsh_hi, 1)
                pool.wait_ge(s_wsh_hi, i + 1)
                pool.tensor_tensor(w_lo, w, w_hi.bitcast(F32), ALU.subtract).then_inc(s_wsh_lo, 1)

            def scatter(b, ks):
                pool.wait_ge(s_dest, b + 1)
                pool.wait_ge(s_w, b + 1)
                if b == 0:
                    pool.wait_ge(s_init, 16)
                for k in ks:
                    pool.indirect_dma_start(
                        out=list_dram[:, :], out_offset=bass.IndirectOffsetOnAxis(ap=dest[:, b, k:k + 1], axis=0),
                        in_=pairs[:, b, k, :], in_offset=None, bounds_check=E * CAP - 1, oob_is_err=False).then_inc(s_scat, 16)

            ln1 = (s_mv1, mv1, s_ve1, ve1, s_rstd1, rstd1)
            ln2 = (s_mv2, mv2, s_ve2, ve2, s_rstd2, rstd2)
            rstd(0, *ln1)
            pool.wait_ge(s_zero, 1)
            pool.memset(qst[0:64, :, :, 1, :].bitcast(F32), 0.0).then_inc(s_zero, 1)
            rstd(1, *ln1)
            pool.wait_ge(s_zero, 2)
            pool.wait_ge(s_rstd1, 2)
            pool.memset(qst[64:P, :, :, 0, :].bitcast(F32), 0.0).then_inc(s_zero, 1)
            pool.wait_ge(s_zero, 3)
            pool.wait_ge(s_cst, 16)
            pool.wait_ge(s_fills0, 2)
            pool.tensor_copy(pairs[:, :, :, 0], cst[:, C_TOKEN:C_TOKEN + B].unsqueeze(2).to_broadcast([P, B, TOPK])).then_inc(s_pconst, 1)
            rstd(2, *ln1)
            low_part(1)
            for t in range(B + 4):
                first = (1 if t < B else 2 if t == B else 0) if t >= 4 else 0
                if first:
                    scatter(t - 4, range(0, first))
                if 0 <= t - 2 < B:
                    rstd(t - 2, *ln2)
                if t >= 4:
                    scatter(t - 4, range(first, 2))
                if t + 3 < B:
                    rstd(t + 3, *ln1)
                if t >= 4:
                    scatter(t - 4, range(2, 4))
                if t + 2 < B:
                    low_part(t + 2)
                if t >= 4:
                    scatter(t - 4, range(4, TOPK))
                else:
                    split_shared(t)

            def gather_rows(e, r):
                if not (isinstance(e, int) and e < RING):
                    pool.wait_ge(s_xps, e - (RING - 1))
                pool.wait_ge(s_tokg, e + 1)
                pool.sem_inc(s_go, 1)
                for t in range(TILES):
                    pool.indirect_dma_start(
                        out=slot[:, r, t, :], out_offset=None, in_=z_dram[:, :],
                        in_offset=bass.IndirectOffsetOnAxis(ap=tok_g[:, r, t:t + 1], axis=0)).then_inc(s_x_in[r], 16)

            def add_rows(e, r, t):
                pool.wait_ge(s_ys[t], e + 1)
                if t == 0:
                    pool.wait_ge(s_toka, e + 1)
                if not (isinstance(e, int) and e == 0):
                    pool.wait_ge(s_acc[t], e * 16)
                pool.sem_inc(s_added[t], 1)
                pool.indirect_dma_start(
                    out=acc_dram[t][:, :], out_offset=bass.IndirectOffsetOnAxis(ap=tok_a[:, r, t:t + 1], axis=0),
                    in_=ysc[:, r, t, :], in_offset=None, compute_op=ALU.add).then_inc(s_acc[t], 16)

            for t in range(TILES):
                pool.sem_inc(s_added[t], RING - 1)
            pool.wait_ge(s_zst, 16 * (B + 1))
            for e in range(RING - 1):
                gather_rows(e, e)
            pool.wait_ge(s_acc0, 32)
            for i in range(2):
                pool.wait_ge(s_seed[i], 16 * B // 2)

            def expert(e, r):
                if not (isinstance(e, int) and e >= E - RING + 1):
                    gather_rows(e + RING - 1, (r - 1) % RING)
                if not (isinstance(e, int) and e == 0):
                    for t in range(TILES):
                        add_rows(e - 1, (r - 1) % RING, t)

            experts(pool, expert)
            for t in range(TILES):
                add_rows(E - 1, (E - 1) % RING, t)

            pool.wait_ge(s_flag, 1)
            n_max = pool.value_load(flag[0:1, 0:1], min_val=0, max_val=TOKENS)
            with pool.If(n_max > TILES * P):
                for t in range(TILES):
                    pool.wait_ge(s_acc[t], 16 * E)
                pool.sem_inc(o_free, 1)
                with pool.Fori(0, E) as e:
                    pool.tensor_copy(tok_g[:, 0, 0:1], slot_tok[:, bass.ds(e * TCAP + TILES, 1)]).then_inc(s_tokg, 1)
                    pool.wait_ge(s_tokg, e + (E + 1))
                    pool.sem_inc(s_go, 1)
                    pool.indirect_dma_start(
                        out=slot[:, 0, 0, :], out_offset=None, in_=z_dram[:, :],
                        in_offset=bass.IndirectOffsetOnAxis(ap=tok_g[:, 0, 0:1], axis=0)).then_inc(s_x_in[0], 16)
                    pool.wait_ge(s_ys[0], e + (E + 1))
                    pool.sem_inc(s_go, 1)
                    pool.indirect_dma_start(
                        out=acc_dram[0][:, :],
                        out_offset=bass.IndirectOffsetOnAxis(ap=tok_g[:, 0, 0:1], axis=0),
                        in_=ysc[:, 0, 0, :], in_offset=None, compute_op=ALU.add).then_inc(s_acc[0], 16)
                    pool.wait_ge(s_acc[0], e * 16 + 16 * (E + 1))
                    pool.sem_inc(o_free, 1)


_INS = ['x', 'ctx_2048', 'g_xattn', 'g_ffn', 'L0_ffn_wg_router', 'L0_ffn_w_gate', 'L0_ffn_w_up', 'L0_ffn_w_down',
        'L0_ffn_ws_gate', 'L0_ffn_ws_up', 'L0_ffn_ws_down']
_OUTS = [((B, P, T), 'float32')]


def _constants():
    import numpy as np
    c = np.zeros((P, C_END), np.float32)
    p = np.arange(P)
    c[:, C_IDENT:C_IDENT + P] = np.eye(P)
    c[:, C_BLOCK:C_BLOCK + P] = p[:, None] // DH == p[None, :] // DH
    c[:, C_TRI:C_TRI + P] = p[:, None] < p[None, :]
    c[:, C_IOTA:C_IOTA + P] = np.arange(P)
    c[:, C_TOKEN:C_TOKEN + B] = np.arange(B) * P + p[:, None]
    c[:, C_ONES_E:C_ONES_E + DH] = 1
    c[:, C_ONES_O + DH:C_ONES_O + 2 * DH] = 1
    c[:, C_FLOOR] = LN_FLOOR
    for i in range(PAIRS):
        k_at, q_at = C_SMALL + i * SELK_W + DH, C_SMALL + PAIRS * SELK_W + i * SELQ_W + 2 * DH
        for a in range(2):
            for d in range(DH):
                row = 2 * DH * i + DH * a + d
                for u in range(2):
                    c[row, k_at + 64 * a + 2 * DH * u + d] = 1
                    c[row, q_at + 64 * a + DH * u + d] = 1
    return c


def kernel(**inputs):
    import numpy as _np
    import concourse.bacc as _bacc
    from concourse import mybir as _mybir
    from concourse.bass_utils import run_bass_kernel_spmd as _run

    nc = _bacc.Bacc("TRN2", target_bir_lowering=False, num_devices=1)
    arrays, args = {}, []
    for name in _INS:
        a = _np.ascontiguousarray(inputs[name])
        arrays[f"in_{name}_dram"] = a
        args.append(nc.dram_tensor(f"in_{name}_dram", a.shape, _mybir.dt.from_np(a.dtype), kind="ExternalInput").ap())
    arrays["consts_dram"] = _constants()
    args.append(nc.dram_tensor("consts_dram", arrays["consts_dram"].shape, _mybir.dt.float32, kind="ExternalInput").ap())
    for i, (shape, dtype) in enumerate(_OUTS):
        args.append(nc.dram_tensor(f"out_{i}_dram", shape, _mybir.dt.from_np(_np.dtype(dtype)), kind="ExternalOutput").ap())
    flamingo_block_kernel(nc, *args)
    r = _run(nc, [arrays], core_ids=[0])
    return r.results[0]["out_0_dram"]
```
